# Optimizing a Trainium2 kernel written in Bass

```python
import numpy as np
import jax
import jax.numpy as jnp

def _softmax(x, axis=-1):
    return jax.nn.softmax(x, axis=axis)
def _gelu(x):
    return jax.nn.gelu(x, approximate=True)
def _silu(x):
    return jax.nn.silu(x)
def _sigmoid(x):
    return jax.nn.sigmoid(x)
def _layernorm(x, axis=-1, eps=1e-5):
    m = jnp.mean(x, axis=axis, keepdims=True)
    v = jnp.var(x, axis=axis, keepdims=True)
    return (x - m) / jnp.sqrt(v + eps)
def _scatter_add(tgt, idx, src, axis=0):
    return tgt.at[idx].add(src)
def _segment_sum(src, seg, n):
    return jax.ops.segment_sum(src, seg, n)

kernel_name = 'mk_vit_tower_cls_d1_tok_img512_d41d87'

def setup_inputs(seed: int = 0):
    np.random.seed(seed)
    _w = jnp.asarray
    def _rec_inputs():
        import jax
        import jax.numpy as jnp
        _rk = jax.random.key(seed)
        x = (-0.000477451 + 1.00034 * jax.random.normal(jax.random.fold_in(_rk, 1), (16, 32, 32, 29), jnp.float32))
        cls_tok = 0.02 * jax.random.normal(jax.random.fold_in(_rk, 5), (1, 1, 512), jnp.float32)
        return x, cls_tok
    x, cls_tok = _rec_inputs()
    def _L0_tok_setup():
        import jax, jax.numpy as jnp
        import numpy as np
        import math
        H, W_DIM, D_MODEL, B = (32, 32, 512, 128)
        F_TOTAL = 29
        SEQ_LEN = H * W_DIM

        def make_pe(seq_len: int, d_model: int) -> jnp.ndarray:
            position = np.arange(seq_len, dtype=np.float32)[:, None]
            div_term = np.exp(np.arange(0, d_model, 2, dtype=np.float32) * (-math.log(10000.0) / d_model))
            pe = np.zeros((seq_len, d_model), dtype=np.float32)
            pe[:, 0::2] = np.sin(position * div_term)
            pe[:, 1::2] = np.cos(position * div_term)
            return jnp.asarray(pe)
        key = jax.random.key(seed)
        k1, k2 = jax.random.split(key)
        state_tensor = jax.random.normal(k1, (B, H, W_DIM, F_TOTAL), dtype=jnp.float32)
        W = jax.random.normal(k2, (F_TOTAL, D_MODEL), dtype=jnp.float32) * 0.05
        return {'state_tensor': state_tensor, 'W': W}
    _L0_tok_all = _L0_tok_setup()
    _L0_tok_in = {k: v for k, v in _L0_tok_all.items() if k in ('W', )}
    del _L0_tok_all

    def _L0_attn_setup():
        import jax, jax.numpy as jnp
        import numpy as np
        D_STATE = 128
        D_MODEL = 512
        key = jax.random.key(seed)
        k1, k2, k3 = jax.random.split(key, 3)
        x = jax.random.normal(k1, (8, 8192, D_MODEL), dtype=jnp.float32)
        log_lambda = -0.5 * jnp.ones((D_STATE,), dtype=jnp.float32)
        B = jax.random.normal(k2, (D_STATE, D_MODEL), dtype=jnp.float32) * 0.05
        C = jax.random.normal(k3, (D_MODEL, D_STATE), dtype=jnp.float32) * 0.05
        log_dt = jnp.asarray(0.0, dtype=jnp.float32)
        return {'x': x, 'log_lambda': log_lambda, 'B': B, 'C': C, 'log_dt': log_dt}
    _L0_attn_all = _L0_attn_setup()
    _L0_attn_in = {k: v for k, v in _L0_attn_all.items() if k in ('log_lambda', 'B', 'C', 'log_dt', )}
    del _L0_attn_all

    def _L0_ffn_setup():
        import jax, jax.numpy as jnp
        import numpy as np
        MARK_AX, OP_ADD, OP_SUB = (0, 1, 2)
        ALU_LO, ALU_HI = (16, 32)
        AX_CARRY_LO, AX_CARRY_HI = (48, 64)
        OPCODE_BASE = 80
        OUTPUT_LO, OUTPUT_HI, CARRY = (128, 144, 160)
        NIB_A, NIB_B, OP_START = (0, 1, 10)
        RESULT, CARRY_OUT = (100, 101)
        GE_POS, GE_DIM = (8, 160)
        OPC_ADD, OPC_SUB = (25, 26)
        B, S, D = (8, 4096, 512)

        def _decode_nibble(x, base):
            return jnp.argmax(x[..., base:base + 16] > 0.5, axis=-1).astype(x.dtype)

        def _pipeline(h, W, b):
            for i in range(3):
                h = jnp.einsum('bspd,od->bspo', h, W[i]) + b[i]
                if i < 2:
                    h = jax.nn.relu(h)
            return h
        key = jax.random.key(seed)
        kx, k1, k2, k3, k4 = jax.random.split(key, 5)
        x_bd = jax.random.uniform(kx, (B, S, D), dtype=jnp.float32)
        Wa = jax.random.normal(k1, (3, GE_DIM, GE_DIM), dtype=jnp.float32) * 0.05
        ba = jax.random.normal(k2, (3, GE_DIM), dtype=jnp.float32) * 0.05
        Ws = jax.random.normal(k3, (3, GE_DIM, GE_DIM), dtype=jnp.float32) * 0.05
        bs = jax.random.normal(k4, (3, GE_DIM), dtype=jnp.float32) * 0.05
        return {'x_bd': x_bd, 'Wa': Wa, 'ba': ba, 'Ws': Ws, 'bs': bs}
    _L0_ffn_all = _L0_ffn_setup()
    _L0_ffn_in = {k: v for k, v in _L0_ffn_all.items() if k in ('Wa', 'ba', 'Ws', 'bs', )}
    del _L0_ffn_all

    return {
        "x": x,
        "cls_tok": cls_tok,
        "L0_tok_W": _L0_tok_in["W"],
        "L0_attn_log_lambda": _L0_attn_in["log_lambda"],
        "L0_attn_B": _L0_attn_in["B"],
        "L0_attn_C": _L0_attn_in["C"],
        "L0_attn_log_dt": _L0_attn_in["log_dt"],
        "L0_ffn_Wa": _L0_ffn_in["Wa"],
        "L0_ffn_ba": _L0_ffn_in["ba"],
        "L0_ffn_Ws": _L0_ffn_in["Ws"],
        "L0_ffn_bs": _L0_ffn_in["bs"],
    }

def reference(x, cls_tok, L0_tok_W, L0_attn_log_lambda, L0_attn_B, L0_attn_C, L0_attn_log_dt, L0_ffn_Wa, L0_ffn_ba, L0_ffn_Ws, L0_ffn_bs):
    import jax
    import jax.numpy as jnp
    def _L0_tok_ref(state_tensor, W):
        import jax, jax.numpy as jnp
        import numpy as np
        import math
        H, W_DIM, D_MODEL, B = (32, 32, 512, 128)
        F_TOTAL = 29
        SEQ_LEN = H * W_DIM

        def make_pe(seq_len: int, d_model: int) -> jnp.ndarray:
            position = np.arange(seq_len, dtype=np.float32)[:, None]
            div_term = np.exp(np.arange(0, d_model, 2, dtype=np.float32) * (-math.log(10000.0) / d_model))
            pe = np.zeros((seq_len, d_model), dtype=np.float32)
            pe[:, 0::2] = np.sin(position * div_term)
            pe[:, 1::2] = np.cos(position * div_term)
            return jnp.asarray(pe)
        b, h, w, f = state_tensor.shape
        s = h * w
        x = state_tensor.reshape(b, s, f)
        emb = jnp.einsum('bsf,fd->bsd', x, W)
        pe = make_pe(s * 2, W.shape[1])[:s]
        return emb + pe[None, :, :]

    def _L0_attn_ref(x, log_lambda, B, C, log_dt):
        import jax, jax.numpy as jnp
        import numpy as np
        D_STATE = 128
        D_MODEL = 512
        T = x.shape[1]
        dt = jnp.exp(log_dt)
        lam = -jnp.exp(log_lambda)
        log_decay = lam * dt
        t_idx = jnp.arange(T, dtype=x.dtype)
        log_decay_t = jnp.clip(t_idx[:, None] * log_decay[None, :], -30.0, 0.0)
        decay_t = jnp.exp(log_decay_t)
        inv_decay_t = jnp.minimum(jnp.exp(-log_decay_t), 1000000.0)
        Bu = jnp.einsum('btd,nd->btn', x, B)
        Bu_scaled = Bu * inv_decay_t[None]
        h_scaled = jnp.cumsum(Bu_scaled, axis=1)
        h_out = h_scaled * decay_t[None]
        return jnp.einsum('btn,dn->btd', h_out, C)

    def _L0_ffn_ref(x_bd, Wa, ba, Ws, bs):
        import jax, jax.numpy as jnp
        import numpy as np
        MARK_AX, OP_ADD, OP_SUB = (0, 1, 2)
        ALU_LO, ALU_HI = (16, 32)
        AX_CARRY_LO, AX_CARRY_HI = (48, 64)
        OPCODE_BASE = 80
        OUTPUT_LO, OUTPUT_HI, CARRY = (128, 144, 160)
        NIB_A, NIB_B, OP_START = (0, 1, 10)
        RESULT, CARRY_OUT = (100, 101)
        GE_POS, GE_DIM = (8, 160)
        OPC_ADD, OPC_SUB = (25, 26)
        B, S, D = (8, 4096, 512)

        def _decode_nibble(x, base):
            return jnp.argmax(x[..., base:base + 16] > 0.5, axis=-1).astype(x.dtype)

        def _pipeline(h, W, b):
            for i in range(3):
                h = jnp.einsum('bspd,od->bspo', h, W[i]) + b[i]
                if i < 2:
                    h = jax.nn.relu(h)
            return h
        x = x_bd
        Bsz, seq, _ = x.shape
        x_ge = jnp.zeros((Bsz, seq, GE_POS, GE_DIM), dtype=x.dtype)
        x_ge = x_ge.at[..., 0, NIB_A].set(_decode_nibble(x, ALU_LO))
        x_ge = x_ge.at[..., 1, NIB_A].set(_decode_nibble(x, ALU_HI))
        x_ge = x_ge.at[..., 0, NIB_B].set(_decode_nibble(x, AX_CARRY_LO))
        x_ge = x_ge.at[..., 1, NIB_B].set(_decode_nibble(x, AX_CARRY_HI))
        x_ge = x_ge.at[..., :, OP_START + OPC_ADD].set(x[..., OPCODE_BASE + OPC_ADD][..., None])
        x_ge = x_ge.at[..., :, OP_START + OPC_SUB].set(x[..., OPCODE_BASE + OPC_SUB][..., None])
        mark = x[..., MARK_AX] > 0.5
        m_add = mark & (x[..., OP_ADD] > 0.5)
        m_sub = mark & ~(x[..., OP_ADD] > 0.5) & (x[..., OP_SUB] > 0.5)
        active = (m_add | m_sub).astype(x.dtype)
        y_add = _pipeline(x_ge, Wa, ba)
        y_sub = _pipeline(x_ge, Ws, bs)
        y = jnp.where(m_add[..., None, None], y_add, jnp.where(m_sub[..., None, None], y_sub, x_ge))
        res_lo = jnp.clip(jnp.round(y[..., 0, RESULT]), 0, 15).astype(jnp.int32)
        res_hi = jnp.clip(jnp.round(y[..., 1, RESULT]), 0, 15).astype(jnp.int32)
        oh_lo = jax.nn.one_hot(res_lo, 16, dtype=x.dtype) * active[..., None]
        oh_hi = jax.nn.one_hot(res_hi, 16, dtype=x.dtype) * active[..., None]
        carry = (jnp.round(y[..., 1, CARRY_OUT]) > 0.5).astype(x.dtype) * active
        out = x
        out = out.at[..., OUTPUT_LO:OUTPUT_LO + 16].add(2.0 * oh_lo)
        out = out.at[..., OUTPUT_HI:OUTPUT_HI + 16].add(2.0 * oh_hi)
        out = out.at[..., CARRY].add(carry)
        return out

    h = _L0_tok_ref(x, L0_tok_W)
    h = jnp.concatenate([jnp.broadcast_to(cls_tok, (h.shape[0], 1, h.shape[2])), h], axis=1)
    h = h + _L0_attn_ref(_layernorm(h, axis=-1), L0_attn_log_lambda, L0_attn_B, L0_attn_C, L0_attn_log_dt)
    h = h + _L0_ffn_ref(_layernorm(h, axis=-1), L0_ffn_Wa, L0_ffn_ba, L0_ffn_Ws, L0_ffn_bs)
    return h


_drawn_inputs = setup_inputs


def setup_inputs(seed=0):
    import zlib

    import numpy as np

    out = dict(_drawn_inputs(seed))
    spreads = {'L0_attn_log_lambda': (-0.5, 0.2)}
    factors = {}
    for name, (base, spread) in spreads.items():
        noise = np.random.default_rng([zlib.crc32(name.encode()), seed]).standard_normal(out[name].shape)
        drawn = base * np.exp(spread * noise) if base else spread * noise
        out[name] = jnp.asarray(drawn.astype(out[name].dtype))
    for name, factor in factors.items():
        out[name] = (out[name] * factor).astype(out[name].dtype)
    return out
```

```python
import math
from contextlib import ExitStack

import numpy as np
import concourse.bass as bass
from concourse import mybir

F32 = mybir.dt.float32
F32R = mybir.dt.float32r
ALU = mybir.AluOpType
ACT = mybir.ActivationFunctionType
AX = mybir.AxisListType


def position_table(seq_len, d_model):
    position = np.arange(seq_len, dtype=np.float32)[:, None]
    div_term = np.exp(np.arange(0, d_model, 2, dtype=np.float32) * (-math.log(10000.0) / d_model))
    pe = np.zeros((seq_len, d_model), dtype=np.float32)
    pe[:, 0::2] = np.sin(position * div_term)
    pe[:, 1::2] = np.cos(position * div_term)
    return pe


def after(eng, sem, count):
    if isinstance(count, int) and count <= 0:
        return
    eng.wait_ge(sem, count)


SU_CENTRED, SU_CLIP, SU_CLSVE, SU_CLSN, SU_BW, SU_CLST, SU_PE, SU_CLSU, SU_ALL = 6, 12, 15, 23, 24, 29, 37, 38, 39
CONSTS = 13
TS_W, TS_C, TS_R, TS_CLST, TS_PE, TS_CLSU, TS_FFN, TS_CLSH = 1, 2, 3, 4, 4, 21, 22, 23


def vit_layer(nc, x, cls_tok, tok_w, log_lambda, B, C, log_dt, Wa, ba, Ws, bs, pe, out):
    P = 128
    BATCH, GRID_H, GRID_W, F = x.shape
    D = tok_w.shape[1]
    NS = B.shape[0]
    TOK = GRID_H * GRID_W
    TPG = 4
    GT = TPG * P
    TILES = TOK // P
    GROUPS = BATCH * TOK // GT
    DC = D // P
    BLK = 32
    NB = P // BLK
    RG = NS + BLK
    GE = Wa.shape[1]
    REM = GE - P
    EPS = 1e-5
    HALF = 0.5
    NIB_A, OPC_ADD, ALU_LO, OP_START = 0, 25, 16, 10
    IN_OP = OP_START + OPC_ADD
    X_OP = 80 + OPC_ADD
    FIELDS, NIB = 4, 16
    YC = X_OP + 2
    RESULT = 100
    OUT_LO, CARRY = 128, 160
    NFEAT = 9
    KF = 2 * 2 * NFEAT
    MAGIC = 1.5 * 2.0 ** 23
    assert D == 512 and NS == P and F <= BLK - 1 and TILES == 2 * TPG and REM == 32

    xf = x.rearrange("b h w f -> (b h w) f")
    pipes = ((Wa, ba), (Ws, bs))

    ctx = ExitStack()
    with ctx:
        def sb(name, shape, dt=F32):
            return ctx.enter_context(nc.sbuf_tensor(name, shape, dt))

        def sem(name):
            return ctx.enter_context(nc.semaphore(name))

        ident = sb("ident", [P, P])
        tri = sb("tri", [P, P])
        pe_sb = sb("pe_sb", [P, TILES, D])
        pe_state = sb("pe_state", [P, TILES, NS])
        pe_var = sb("pe_var", [P, TILES, BLK])
        var_pe = sb("var_pe", [P, TILES, 2])
        decayT = sb("decayT", [P, TOK])
        inv_decay = sb("inv_decay", [P, TILES, NS])
        w_x = sb("w_x", [P, D], F32R)
        r_x = sb("r_x", [P, RG], F32R)
        CT = sb("CT", [P, D])
        w_feat = sb("w_feat", [KF, 8, P], F32R)
        w2_main = sb("w2_main", [P, 2, P])
        w2_main_rem = sb("w2_main_rem", [P, 2, REM])
        w2_rem_main = sb("w2_rem_main", [P, 2, P])
        w2_rem = sb("w2_rem", [P, P])
        w3 = sb("w3", [P, 3, 6])
        b3 = sb("b3", [P, 6])
        nib_w = sb("nib_w", [P, FIELDS, NIB])
        hot = sb("hot", [P, NIB])
        ones4 = sb("ones4", [P, TPG])
        carry_cls = sb("carry_cls", [P, 1])
        B_sb = sb("B_sb", [P, D])
        C_sb = sb("C_sb", [P, DC, P])
        W4 = sb("W4", [P, D])
        W4c = sb("W4c", [P, D])
        w_hi = sb("w_hi", [P, D], F32R)
        r_all = sb("r_all", [P, RG])
        r_hi = sb("r_hi", [P, RG], F32R)
        BW = sb("BW", [P, DC, RG])
        W4T = sb("W4T", [P, DC, P])
        peT = sb("peT", [P, 2, D])
        mean_b = sb("mean_b", [P, 1])
        mean_w = sb("mean_w", [P, 1])
        stat_pe = sb("stat_pe", [P, TILES, 6])
        ll_col = sb("ll_col", [P, 2])
        ll_row = sb("ll_row", [P, NS])
        ld_col = sb("ld_col", [P, 1])
        ld_row = sb("ld_row", [P, NS])
        t_row = sb("t_row", [P, TOK])
        t_col = sb("t_col", [P, TILES])
        top1 = sb("top1", [P, 2, GE])
        bot1 = sb("bot1", [REM, 2, GE])
        diag1 = sb("diag1", [P, P])
        spread1 = sb("spread1", [P, 2, P])
        top0 = sb("top0", [P, 2, GE])
        rem0 = sb("rem0", [P, GE])
        bias_main = sb("bias_main", [P, 2, 2])
        bias_rem = sb("bias_rem", [P, 2])
        zf = sb("zf", [P, 8, 2, NFEAT])
        zr = sb("zr", [P, 8, 2, 2, NFEAT], F32R)
        cls_sb = sb("cls_sb", [P, D])
        cls_st = sb("cls_st", [P, 6])
        cls_mv = sb("cls_mv", [P, 2])
        cls_ve = sb("cls_ve", [P, 1])
        cls_sd = sb("cls_sd", [P, 1])
        cls_r = sb("cls_r", [P, 4])
        cls_n = sb("cls_n", [P, D])
        clsT = sb("clsT", [P, D])
        stateT_cls = sb("stateT_cls", [P, P])
        x_in = sb("x_in", [P, 2, TPG, F])
        x_parts = sb("x_parts", [P, 2, TPG, NB, BLK], F32R)
        xT = sb("xT", [P, 2, GT], F32R)
        q_prod = sb("q_prod", [P, TPG, F])
        q_sum = sb("q_sum", [P, TPG])
        ve1 = sb("ve1", [P, TPG])
        sd1 = sb("sd1", [P, TPG])
        rs1 = sb("rs1", [P, 4, TPG])
        state_raw = sb("state_raw", [P, TPG, NS])
        state_in = sb("state_in", [P, TPG, NS])
        carry = sb("carry", [P, 2, TPG])
        stateT = sb("stateT", [P, 2, GT])
        h1 = sb("h1", [P, 2, TPG, D])
        st2 = sb("st2", [P, TPG, 6])
        mv2 = sb("mv2", [P, TPG, 2])
        ve2 = sb("ve2", [P, TPG])
        sd2 = sb("sd2", [P, TPG])
        rs2 = sb("rs2", [P, 4, TPG])
        out_scale = sb("out_scale", [P, 2, TPG])
        out_bias = sb("out_bias", [P, 2, TPG])
        y = sb("y", [P, TPG, YC])
        first_hit = sb("first_hit", [P, TPG, FIELDS, NIB])
        hit_max = sb("hit_max", [P, TPG, FIELDS])
        hit_pos = sb("hit_pos", [P, TPG, FIELDS])
        marks = sb("marks", [P, TPG, 3])
        both = sb("both", [P, TPG, 2])
        masks = sb("masks", [P, 2, TPG, 2])
        active = sb("active", [P, 2, TPG])
        feat = sb("feat", [P, TPG, NFEAT], F32R)
        feat_rows = sb("feat_rows", [P, TPG, P], F32R)
        featT = sb("featT", [KF, GT], F32R)
        hid1 = sb("hid1", [P, 5, GT])
        hid2 = sb("hid2", [P, 3, GT])
        y3 = sb("y3", [P, TPG, 6])
        y3m = sb("y3m", [P, TPG, 6])
        res = sb("res", [P, TPG, 3])
        res_c = sb("res_c", [P, TPG, 2])
        res_up = sb("res_up", [P, TPG, 2])
        res_int = sb("res_int", [P, TPG, 2])
        is_hot = sb("is_hot", [P, TPG, 2, NIB])
        is_hot2 = sb("is_hot2", [P, TPG, 2, NIB])
        carry_out = sb("carry_out", [P, TPG])
        o_sb = sb("o_sb", [P, 2, TPG, D])

        bank = [ctx.enter_context(nc.psum_tensor(f"bank{n}", [P, 512], F32)) for n in range(8)]
        ps_T, ps_small, ps_state, ps_scan = bank[0], bank[1], bank[2], bank[3]
        ps_h, ps_f = bank[4:6], bank[6:8]
        ps_var = ps_small[:, 0:TPG * BLK].rearrange("p (c k) -> p c k", c=TPG)
        ps_y = ps_small[:, 256:256 + TPG * 6].rearrange("p (c k) -> p c k", c=TPG)
        state_v = ps_state[:, :].rearrange("p (c k) -> p c k", c=TPG)

        ld_b, ld_w, ld_c, ld_pe, ld_lam, ld_cls = (sem(n) for n in ("ld_b", "ld_w", "ld_c", "ld_pe", "ld_lam", "ld_cls"))
        ld_f1, ld_f0, ld_f3 = sem("ld_f1"), sem("ld_f0"), sem("ld_f3")
        zeroed = sem("zeroed")
        const_step = sem("const_step")
        su_v = sem("su_v")
        su_a = sem("su_a")
        su_t = sem("su_t")
        spread_done = sem("spread_done")
        x_loaded = [sem("x_loaded0"), sem("x_loaded1")]
        x_hi = sem("x_hi")
        x_split, xT_ready, xT_copied = sem("x_split"), sem("xT_ready"), sem("xT_copied")
        var_ready, var_read, state_ready, state_read = sem("var_ready"), sem("var_read"), sem("state_ready"), sem("state_read")
        v1 = [sem(f"v1_{n}") for n in range(8)]
        sd1_ready = sem("sd1_ready")
        state_scaled, scan_ready, carry_ready, stateT_ready = sem("state_scaled"), sem("scan_ready"), sem("carry_ready"), sem("stateT_ready")
        h_ready = [sem(f"h_ready{c}") for c in range(TPG)]
        h_added = [sem(f"h_added{c}") for c in range(TPG)]
        h_stat, h_aggr = sem("h_stat"), sem("h_aggr")
        v2 = [sem(f"v2_{n}") for n in range(5)]
        ve2_ready, sd2_ready, scale_ready = sem("ve2_ready"), sem("sd2_ready"), sem("scale_ready")
        y_done, hits_done, max_done, pos_done, op_hi_done, marks_done, both_done, masks_done, feat_done = (
            sem(n) for n in ("y_done", "hits_done", "max_done", "pos_done", "op_hi_done", "marks_done",
                             "both_done", "masks_done", "feat_done"))
        rows_ready, featT_ready, featT_copied = sem("rows_ready"), sem("featT_ready"), sem("featT_copied")
        f_ready = [sem(f"f_ready{k}") for k in range(8)]
        f_relu = [sem(f"f_relu{k}") for k in range(8)]
        y3_ready, y3_read = sem("y3_ready"), sem("y3_read")
        p3 = [sem(f"p3_{n}") for n in range(8)]
        o_scaled, o_done = sem("o_scaled"), sem("o_done")
        o_stored = [sem("o_stored0"), sem("o_stored1")]

        block = ctx.enter_context(nc.Block())

        def load_x(eng, g, row, par):
            after(eng, x_split, g - 2)
            after(eng, v1[1], g - 2)
            eng.dma_start(x_in[:, par, :, :], xf[bass.ds(row, GT), :].rearrange("(c p) f -> p c f", p=P)
                          ).then_inc(x_loaded[par], 16)

        def store(eng, g, b, half, par):
            after(eng, o_done, g + 1)
            eng.dma_start(out[b, 1 + half * GT:1 + (half + 1) * GT, :].rearrange("(c p) d -> p c d", p=P),
                          o_sb[:, par, :, :]).then_inc(o_stored[par], 16)

        @block.sync
        def _(sp):
            sp.dma_start(B_sb[:, :], B).then_inc(ld_b, 16)
            sp.wait_ge(zeroed, 1)
            for n in range(NB):
                sp.dma_start(W4[n * BLK:n * BLK + F, :], tok_w).then_inc(ld_w, 16)
            sp.dma_start(pe_sb[:, :, :], pe.rearrange("(c p) d -> p c d", p=P)).then_inc(ld_pe, 16)
            sp.dma_start(cls_sb[:, :], cls_tok[0, :, :].to_broadcast([P, D])).then_inc(ld_cls, 16)
            load_x(sp, 1, 0, 1)
            load_x(sp, 2, GT, 0)
            sp.wait_ge(o_done, 1)
            sp.dma_start(out[:, 0, :], o_sb[0:BATCH, 0, 0, :]).then_inc(o_stored[0], 16)
            load_x(sp, 3, 2 * GT, 1)
            store(sp, 1, 0, 0, 1)
            load_x(sp, 4, 3 * GT, 0)
            store(sp, 2, 0, 1, 0)
            with sp.Fori(1, BATCH - 1) as b:
                for half in range(2):
                    load_x(sp, 2 * b + 3 + half, (2 * b + 2 + half) * GT, 1 - half)
                    store(sp, 2 * b + 1 + half, b, half, 1 - half)
            store(sp, GROUPS - 1, BATCH - 1, 0, 1)
            store(sp, GROUPS, BATCH - 1, 1, 0)
            sp.wait_ge(o_stored[1], 16 * BATCH)
            sp.wait_ge(o_stored[0], 16 * (BATCH + 1))

        @block.gpsimd
        def _(pool):
            g = nc.gpsimd
            g.memset(W4[:, :], 0.0).then_inc(zeroed, 1)
            g.memset(diag1[:, :], 0.0).then_inc(zeroed, 1)
            g.memset(w3[:, :, :], 0.0).then_inc(zeroed, 1)
            g.memset(ident[:, :], 0.0).then_inc(const_step, 1)
            g.memset(tri[:, :], 1.0).then_inc(const_step, 1)
            pool.wait_ge(const_step, 2)
            g.affine_select(out=ident[:, :], in_=ident[:, :], compare_op=ALU.not_equal, fill=1.0, base=0,
                            pattern=[[-1, P]], channel_multiplier=1).then_inc(const_step, 1)
            g.affine_select(out=tri[:, :], in_=tri[:, :], compare_op=ALU.is_ge, fill=0.0, base=0,
                            pattern=[[1, P]], channel_multiplier=-1).then_inc(const_step, 1)
            imp = dict(allow_small_or_imprecise_dtypes=True)
            g.iota(t_row[:, :], pattern=[[1, TOK]], base=1, channel_multiplier=0, **imp).then_inc(const_step, 1)
            g.iota(t_col[:, :], pattern=[[P, TILES]], base=1, channel_multiplier=1, **imp).then_inc(const_step, 1)
            g.iota(nib_w[:, :, :], pattern=[[0, FIELDS], [-1, NIB]], base=NIB, channel_multiplier=0, **imp).then_inc(const_step, 1)
            g.iota(hot[:, :], pattern=[[1, NIB]], base=0, channel_multiplier=0, **imp).then_inc(const_step, 1)
            g.memset(x_parts[:, :, :, :, :].bitcast(F32), 0.0).then_inc(const_step, 1)
            g.memset(zf[:, :, :, :], 0.0).then_inc(const_step, 1)
            g.memset(spread1[:, :, :], 0.0).then_inc(const_step, 1)
            g.memset(ones4[:, :], 1.0).then_inc(const_step, 1)
            g.memset(feat_rows[:, :, :].bitcast(F32), 0.0).then_inc(const_step, 1)
            pool.wait_ge(const_step, CONSTS)

            def split_x(n, par):
                after(pool, x_loaded[par], 16 * n["load"])
                after(pool, xT_ready, n["g"] - 2)
                parts, xin = x_parts[:, par, :, :, :], x_in[:, par, :, :]
                g.tensor_tensor(parts[:, :, 0, 0:F], xin, ones4[:, :].unsqueeze(2).to_broadcast([P, TPG, F]), ALU.mult).then_inc(x_hi, 1)
                g.tensor_copy(parts[:, :, 2, 0:F], xin).then_inc(x_hi, 1)
                after(pool, x_hi, 2 * n["g"])
                g.tensor_tensor(parts[:, :, 1, 0:F], xin, parts[:, :, 0, 0:F].bitcast(F32), ALU.subtract)
                g.tensor_tensor(parts[:, :, 3, 0:F], xin, parts[:, :, 0, 0:F].bitcast(F32), ALU.subtract
                                ).then_inc(x_split, 1)

            split_x(dict(g=1, load=1), 1)
            split_x(dict(g=2, load=1), 0)
            split_x(dict(g=3, load=2), 1)
            split_x(dict(g=4, load=2), 0)
            with pool.Fori(1, BATCH - 1) as b:
                for half in range(2):
                    split_x(dict(g=2 * b + 3 + half, load=b + 2), 1 - half)

        @block.scalar
        def _(act):
            a = nc.scalar
            act.dma_start(ll_col[:, 0:1], log_lambda.unsqueeze(1)).then_inc(ld_lam, 16)
            act.dma_start(ll_row[:, :], log_lambda.unsqueeze(0).to_broadcast([P, NS])).then_inc(ld_lam, 16)
            act.dma_start(ll_col[:, 1:2], log_dt.unsqueeze(0).to_broadcast([P, 1])).then_inc(ld_lam, 16)
            act.dma_start(C_sb[:, :, :], C.rearrange("(c p) n -> p c n", p=P)).then_inc(ld_c, 16)
            for m, (w, bb) in enumerate(pipes):
                act.dma_start(top1[:, m, :], w[1, 0:P, :]).then_inc(ld_f1, 16)
                act.dma_start(bot1[:, m, :], w[1, P:GE, :]).then_inc(ld_f1, 16)
                act.dma_start(top0[:, m, :], w[0, 0:P, :]).then_inc(ld_f0, 16)
                act.dma_start(bias_main[:, :, m:m + 1], bb[0:2, 0:P].rearrange("l (p o) -> p l o", o=1), allow_slow_non_contiguous=True).then_inc(ld_f0, 16)
            act.wait_ge(zeroed, 3)
            for q in range(2):
                for m, (w, bb) in enumerate(pipes):
                    r = slice(REM * (2 * q + m), REM * (2 * q + m + 1))
                    act.dma_start(diag1[r, r], w[1, P:GE, P:GE]).then_inc(ld_f1, 16)
                    act.dma_start(rem0[r, :], w[0, P:GE, :]).then_inc(ld_f0, 16)
                    act.dma_start(bias_rem[r, :].unsqueeze(2), bb[0:2, P:GE].rearrange("l (p o) -> p l o", o=1), allow_slow_non_contiguous=True).then_inc(ld_f0, 16)
            for m, (w, bb) in enumerate(pipes):
                for o, row, q in ((0, RESULT, 0), (1, RESULT, 1), (2, RESULT + 1, 1)):
                    col = 2 * o + m
                    r = slice(REM * (2 * q + m), REM * (2 * q + m + 1))
                    act.dma_start(w3[:, q, col:col + 1], w[2, row, 0:P].unsqueeze(1), allow_slow_non_contiguous=True).then_inc(ld_f3, 16)
                    act.dma_start(w3[r, 2, col:col + 1], w[2, row, P:GE].unsqueeze(1), allow_slow_non_contiguous=True).then_inc(ld_f3, 16)
                    act.dma_start(b3[:, col:col + 1], bb[2, row:row + 1].unsqueeze(0).to_broadcast([P, 1]), allow_slow_non_contiguous=True).then_inc(ld_f3, 16)
            act.wait_ge(ld_lam, 48)
            a.activation(ll_col[:, :], ll_col[:, :], ACT.Exp).then_inc(su_a, 1)
            a.activation(ll_row[:, :], ll_row[:, :], ACT.Exp).then_inc(su_a, 1)
            act.wait_ge(su_v, SU_CLIP)
            a.activation(decayT[:, :], decayT[:, :], ACT.Exp).then_inc(su_a, 1)
            a.activation(inv_decay[:, :, :], inv_decay[:, :, :], ACT.Exp, scale=-1.0).then_inc(su_a, 1)
            act.wait_ge(su_v, SU_CLSVE)
            a.activation(cls_sd[:, :], cls_ve[:, :], ACT.Sqrt).then_inc(su_a, 1)
            act.wait_ge(su_t, TS_C)
            a.copy(CT[:, :], bank[3][:, :]).then_inc(su_a, 1)
            for c in range(TILES):
                act.wait_ge(su_t, TS_PE + 2 * c + 1)
                a.copy(peT[:, c % 2, :], bank[4 + c % 2][:, :]).then_inc(su_a, 1)

            def copy_featT(s):
                n = P if isinstance(s, int) and s == 0 else GT
                act.wait_ge(featT_ready, s + 1)
                a.copy(featT[:, 0:n], ps_T[0:KF, 0:n]).then_inc(featT_copied, 1)

            def relu(s, k):
                n = P if isinstance(s, int) and s == 0 else GT
                act.wait_ge(f_ready[k], s + 1)
                dst = hid1[:, k, 0:n] if k < 5 else hid2[:, k - 5, 0:n]
                a.activation(dst, ps_f[k % 2][:, 0:n], ACT.Relu).then_inc(f_relu[k], 1)

            def copy_xT(g, par):
                act.wait_ge(xT_ready, g)
                after(act, h_ready[TPG - 1], g - 2)
                a.copy(xT[:, par, :], ps_T[:, :]).then_inc(xT_copied, 1)

            def sqrt1(g):
                act.wait_ge(v1[3], g)
                a.activation(sd1[:, :], ve1[:, :], ACT.Sqrt).then_inc(sd1_ready, 1)

            def sqrt2(g, nt):
                act.wait_ge(ve2_ready, g + 1)
                a.activation(sd2[:, 0:nt], ve2[:, 0:nt], ACT.Sqrt).then_inc(sd2_ready, 1)

            def scale_out(s, par, tiles, nstore, last):
                act.wait_ge(scale_ready, s + 1)
                after(act, o_stored[par], 16 * nstore)
                for c in tiles:
                    ins = a.activation(o_sb[:, par, c, :], h1[:, par, c, :], ACT.Identity,
                                       bias=out_bias[:, par, c:c + 1], scale=out_scale[:, par, c:c + 1])
                if last:
                    ins.then_inc(o_scaled, 1)

            def step(s, par, nstore, early=True, mid=True):
                cls = isinstance(s, int) and s == 0
                copy_featT(s)
                for k in range(5):
                    relu(s, k)
                scale_out(s, par, range(1 if cls else 2), nstore, cls)
                if early:
                    copy_xT(s + 2, par)
                if mid:
                    sqrt2(s + 1, TPG)
                relu(s, 5)
                if early:
                    sqrt1(s + 2)
                if not cls:
                    scale_out(s, par, range(2, TPG), nstore, True)
                relu(s, 6)
                relu(s, 7)

            copy_xT(1, 1)
            sqrt1(1)
            sqrt2(0, 1)
            step(0, 0, 0)
            step(1, 1, 0)
            step(2, 0, 1)
            with act.Fori(1, BATCH - 1) as b:
                step(2 * b + 1, 1, b)
                step(2 * b + 2, 0, b + 1)
            step(GROUPS - 1, 1, BATCH - 1, early=False)
            step(GROUPS, 0, BATCH, early=False, mid=False)

        @block.vector
        def _(dve):
            v = nc.vector
            done = [0]

            def su(ins):
                done[0] += 1
                ins.then_inc(su_v, 1)
                dve.wait_ge(su_v, done[0])

            dve.wait_ge(ld_b, 16)
            su(v.reduce_sum(mean_b[:, :], B_sb[:, :], axis=AX.X))
            su(v.tensor_scalar(mean_b[:, :], mean_b[:, :], 1.0 / D, None, ALU.mult))
            su(v.tensor_scalar(B_sb[:, :], B_sb[:, :], mean_b[:, 0:1], None, ALU.subtract))
            dve.wait_ge(ld_w, 16 * NB)
            su(v.reduce_sum(mean_w[:, :], W4[:, :], axis=AX.X))
            su(v.tensor_scalar(mean_w[:, :], mean_w[:, :], 1.0 / D, None, ALU.mult))
            su(v.tensor_scalar(W4c[:, :], W4[:, :], mean_w[:, 0:1], None, ALU.subtract))
            assert done[0] == SU_CENTRED
            dve.wait_ge(su_a, 2)
            dve.wait_ge(const_step, CONSTS)
            su(v.tensor_scalar(ld_col[:, :], ll_col[:, 0:1], ll_col[:, 1:2], -1.0, ALU.mult, ALU.mult))
            su(v.tensor_scalar(ld_row[:, :], ll_row[:, :], ll_col[:, 1:2], -1.0, ALU.mult, ALU.mult))
            su(v.tensor_scalar(decayT[:, :], t_row[:, :], ld_col[:, 0:1], -30.0, ALU.mult, ALU.max))
            su(v.tensor_scalar(decayT[:, :], decayT[:, :], 0.0, None, ALU.min))
            for c in range(TILES):
                ins = v.tensor_scalar(inv_decay[:, c, :], ld_row[:, :], t_col[:, c:c + 1], -30.0, ALU.mult, ALU.max)
            su(ins)
            su(v.tensor_scalar(inv_decay[:, :, :], inv_decay[:, :, :], 0.0, None, ALU.min))
            assert done[0] == SU_CLIP
            dve.wait_ge(ld_cls, 16)
            su(v.bn_stats(cls_st[:, :], cls_sb[:, :]))
            su(v.bn_aggr(cls_mv[:, :], cls_st[:, :]))
            su(v.tensor_scalar(cls_ve[:, :], cls_mv[:, 1:2], EPS, None, ALU.add))
            assert done[0] == SU_CLSVE
            dve.wait_ge(ld_pe, 16)
            for c in range(TILES):
                ins = v.bn_stats(stat_pe[:, c, :], pe_sb[:, c, :])
            su(ins)
            for c in range(TILES):
                ins = v.bn_aggr(var_pe[:, c, :], stat_pe[:, c, :])
            su(ins)
            dve.wait_ge(su_a, 5)
            su(v.tensor_scalar(inv_decay[:, :, :], inv_decay[:, :, :], 1e6, None, ALU.min))
            su(v.reciprocal(cls_r[:, 0:1], cls_sd[:, :]))
            su(v.tensor_tensor(cls_r[:, 1:2], cls_r[:, 0:1], cls_r[:, 0:1], ALU.mult))
            su(v.scalar_tensor_tensor(cls_r[:, 2:3], cls_r[:, 1:2], -0.5, cls_ve[:, :], ALU.mult, ALU.mult))
            su(v.scalar_tensor_tensor(cls_r[:, 3:4], cls_r[:, 2:3], 1.5, cls_r[:, 0:1], ALU.add, ALU.mult))
            su(v.tensor_scalar(cls_n[:, :], cls_sb[:, :], cls_mv[:, 0:1], cls_r[:, 3:4], ALU.subtract, ALU.mult))
            assert done[0] == SU_CLSN
            dve.wait_ge(ld_f1, 16 * 8)
            dve.wait_ge(ld_f0, 16 * 12)
            for q in range(2):
                for m in range(2):
                    k, r = 2 * q + m, slice(REM * (2 * q + m), REM * (2 * q + m + 1))
                    v.tensor_copy(spread1[:, q, REM * k:REM * (k + 1)], top1[:, m, P:GE])
                    v.tensor_copy(zf[:, k, m, q:q + 3:2], top0[:, m, 0:2])
                    v.tensor_copy(zf[:, k, m, 4:8].rearrange("p (o d) -> p o d", d=2),
                                  top0[:, m, IN_OP:IN_OP + 2].unsqueeze(2).to_broadcast([P, 2, 2]))
                    v.tensor_copy(zf[:, k, m, 8:9], bias_main[:, 0, m:m + 1])
                    v.tensor_copy(zf[:, 5 + q, m, 8:9], bias_main[:, 1, m:m + 1])
                    v.tensor_copy(zf[r, 4, m, q:q + 3:2], rem0[r, 0:2])
                    v.tensor_copy(zf[r, 4, m, 4:8].rearrange("p (o d) -> p o d", d=2),
                                  rem0[r, IN_OP:IN_OP + 2].unsqueeze(2).to_broadcast([REM, 2, 2]))
                    v.tensor_copy(zf[r, 4, m, 8:9], bias_rem[r, 0:1])
                    v.tensor_copy(zf[r, 7, m, 8:9], bias_rem[r, 1:2]).then_inc(spread_done, 1)
            dve.wait_ge(spread_done, 4)
            v.tensor_copy(zr[:, :, :, 0, :], zf[:, :, :, :]).then_inc(spread_done, 1)
            dve.wait_ge(spread_done, 5)
            v.tensor_tensor(zr[:, :, :, 1, :], zf[:, :, :, :], zr[:, :, :, 0, :].bitcast(F32),
                            ALU.subtract).then_inc(spread_done, 1)
            dve.wait_ge(su_t, TS_W)
            v.tensor_copy(BW[:, :, 0:NS], bank[0][:, :].rearrange("p (c k) -> p c k", c=DC))
            v.tensor_copy(BW[:, :, NS:RG], bank[1][:, :].rearrange("p (c k) -> p c k", c=DC)[:, :, 0:BLK])
            su(v.tensor_copy(W4T[:, :, :], bank[1][:, :].rearrange("p (c k) -> p c k", c=DC)))
            assert done[0] == SU_BW
            v.tensor_copy(w_hi[:, :], W4[:, :])
            su(v.tensor_copy(w_x[0:64, :], W4[0:64, :]))
            v.tensor_tensor(w_x[64:P, :], W4[64:P, :], w_hi[64:P, :].bitcast(F32), ALU.subtract)
            dve.wait_ge(su_t, TS_R)
            su(v.tensor_copy(r_all[:, :], bank[2][:, 0:RG]))
            v.tensor_copy(r_hi[:, :], r_all[:, :])
            su(v.tensor_copy(r_x[0:64, :], r_all[0:64, :]))
            su(v.tensor_tensor(r_x[64:P, :], r_all[64:P, :], r_hi[64:P, :].bitcast(F32), ALU.subtract))
            dve.wait_ge(su_t, TS_CLST)
            su(v.tensor_copy(clsT[:, :], bank[0][:, :]))
            assert done[0] == SU_CLST
            for c in range(TILES):
                dve.wait_ge(su_t, TS_PE + 2 * c + 2)
                v.tensor_copy(pe_state[:, c, :], bank[6 + c % 2][:, 0:NS])
                su(v.tensor_scalar(pe_var[:, c, :], bank[6 + c % 2][:, NS:RG], 2.0, None, ALU.mult))
            assert done[0] == SU_PE
            dve.wait_ge(su_t, TS_CLSU)
            v.tensor_copy(stateT_cls[:, :], bank[1][:, 0:P])
            su(v.tensor_copy(carry_cls[:, :], bank[1][:, 0:1]))
            assert done[0] == SU_CLSU
            dve.wait_ge(su_t, TS_FFN)
            v.tensor_copy(w2_main[:, :, :], bank[3][:, 0:2 * P].rearrange("p (m k) -> p m k", m=2))
            v.tensor_copy(w2_main_rem[:, :, :], bank[3][:, 256:256 + 2 * REM].rearrange("p (m k) -> p m k", m=2))
            v.tensor_copy(w2_rem_main[:, :, :], bank[4][:, 0:2 * P].rearrange("p (m k) -> p m k", m=2))
            v.tensor_copy(w2_rem[:, :], bank[5][:, 0:P])
            v.tensor_copy(w_feat[:, 0:4, :], bank[6][0:KF, :].rearrange("p (m k) -> p m k", m=4))
            v.tensor_copy(w_feat[:, 4:8, :], bank[7][0:KF, :].rearrange("p (m k) -> p m k", m=4))
            dve.wait_ge(su_t, TS_CLSH)
            su(v.tensor_tensor(h1[:, 0, 0, :], bank[2][:, :], cls_sb[:, :], ALU.add))
            assert done[0] == SU_ALL

            def rstd(sems, n, t, sd, ve, nt):
                v.reciprocal(t[:, 0, 0:nt], sd).then_inc(sems[0], 1)
                dve.wait_ge(sems[0], n)
                v.tensor_tensor(t[:, 1, 0:nt], t[:, 0, 0:nt], t[:, 0, 0:nt], ALU.mult).then_inc(sems[1], 1)
                dve.wait_ge(sems[1], n)
                v.scalar_tensor_tensor(t[:, 2, 0:nt], t[:, 1, 0:nt], -0.5, ve, ALU.mult, ALU.mult).then_inc(sems[2], 1)
                dve.wait_ge(sems[2], n)
                v.scalar_tensor_tensor(t[:, 3, 0:nt], t[:, 2, 0:nt], 1.5, t[:, 0, 0:nt], ALU.add, ALU.mult
                                       ).then_inc(sems[3], 1)
                dve.wait_ge(sems[3], n)

            def early_a(g, par, tile0):
                dve.wait_ge(var_ready, g)
                v.tensor_tensor(q_prod[:, :, :], ps_var[:, :, 0:F], pe_var[:, tile0:tile0 + TPG, 0:F], ALU.add
                                ).then_inc(var_read, 1)
                dve.wait_ge(var_read, g)
                v.tensor_tensor(q_prod[:, :, :], q_prod[:, :, :], x_in[:, par, :, :], ALU.mult).then_inc(v1[1], 1)
                dve.wait_ge(v1[1], g)
                v.reduce_sum(q_sum[:, :], q_prod[:, :, :], axis=AX.X).then_inc(v1[0], 1)
                dve.wait_ge(v1[0], g)
                v.scalar_tensor_tensor(ve1[:, :], q_sum[:, :], 1.0 / D, var_pe[:, tile0:tile0 + TPG, 1], ALU.mult, ALU.add
                                       ).then_inc(v1[2], 1)
                dve.wait_ge(v1[2], g)
                v.tensor_scalar(ve1[:, :], ve1[:, :], 0.0, EPS, ALU.max, ALU.add).then_inc(v1[3], 1)
                dve.wait_ge(state_ready, g)
                v.tensor_tensor(state_raw[:, :, :], state_v, pe_state[:, tile0:tile0 + TPG, :], ALU.add
                                ).then_inc(state_read, 1)
                dve.wait_ge(sd1_ready, g)
                dve.wait_ge(state_read, g)
                rstd(v1[4:8], g, rs1, sd1[:, :], ve1[:, :], TPG)
                after(dve, scan_ready, g - 1)
                for c in range(TPG):
                    ins = v.scalar_tensor_tensor(state_in[:, c, :], state_raw[:, c, :], rs1[:, 3, c:c + 1],
                                                 inv_decay[:, tile0 + c, :], ALU.mult, ALU.mult)
                ins.then_inc(state_scaled, 1)

            def early_b(g, par, tile0):
                start = carry_cls[:, 0:1] if par else carry[:, 1, TPG - 1:TPG]
                dve.wait_ge(scan_ready, g)
                v.tensor_tensor_scan(carry[:, par, :], ones4[:, :], ps_scan[:, P - 1:GT:P], start, ALU.mult, ALU.add
                                     ).then_inc(carry_ready, 1)
                dve.wait_ge(carry_ready, g)
                after(dve, h_ready[TPG - 1], g - 2)
                for c in range(TPG):
                    ins = v.scalar_tensor_tensor(stateT[:, par, c * P:(c + 1) * P], ps_scan[:, c * P:(c + 1) * P],
                                                 start if c == 0 else carry[:, par, c - 1:c],
                                                 decayT[:, (tile0 + c) * P:(tile0 + c + 1) * P], ALU.add, ALU.mult)
                ins.then_inc(stateT_ready, 1)

            def mid_h(g, par, tile0):
                after(dve, o_scaled, g - 1)
                for c in range(TPG):
                    dve.wait_ge(h_ready[c], g)
                    v.tensor_tensor(h1[:, par, c, :], ps_h[c % 2][:, :], pe_sb[:, tile0 + c, :], ALU.add
                                    ).then_inc(h_added[c], 1)
                    if c:
                        v.bn_stats(st2[:, c - 1, :], h1[:, par, c - 1, :])
                    if c < TPG - 1:
                        dve.wait_ge(h_added[c], g)
                dve.wait_ge(h_added[TPG - 1], g)
                v.bn_stats(st2[:, TPG - 1, :], h1[:, par, TPG - 1, :]).then_inc(h_stat, 1)

            def mid_f(g, par, nt, first):
                n, T = g + 1, slice(0, nt)
                if first:
                    v.bn_stats(st2[:, 0, :], h1[:, par, 0, :]).then_inc(h_aggr, 1)
                    dve.wait_ge(h_aggr, 1)
                else:
                    dve.wait_ge(h_stat, g)
                v.memset(feat[:, T, NFEAT - 1:NFEAT].bitcast(F32), 1.0)
                for c in range(nt):
                    ins = v.bn_aggr(mv2[:, c, :], st2[:, c, :])
                ins.then_inc(v2[4], 1)
                dve.wait_ge(v2[4], n)
                v.tensor_scalar(ve2[:, T], mv2[:, T, 1], EPS, None, ALU.add).then_inc(ve2_ready, 1)
                dve.wait_ge(sd2_ready, n)
                rstd(v2[0:4], n, rs2, sd2[:, T], ve2[:, T], nt)
                v.tensor_scalar(out_scale[:, par, T], rs2[:, 3, T], 1.0, None, ALU.add)
                v.scalar_tensor_tensor(out_bias[:, par, T], mv2[:, T, 0], -1.0, rs2[:, 3, T], ALU.mult, ALU.mult
                                       ).then_inc(scale_ready, 1)
                for c in range(nt):
                    ins = v.tensor_scalar(y[:, c, :], h1[:, par, c, 0:YC], mv2[:, c, 0:1], rs2[:, 3, c:c + 1],
                                          ALU.subtract, ALU.mult)
                ins.then_inc(y_done, 1)
                dve.wait_ge(y_done, n)
                fields = y[:, T, ALU_LO:ALU_LO + FIELDS * NIB]
                weights = nib_w[:, :, :].rearrange("p f k -> p (f k)").unsqueeze(1).to_broadcast([P, nt, FIELDS * NIB])
                v.scalar_tensor_tensor(first_hit[:, T, :, :].rearrange("p c f k -> p c (f k)"), fields, HALF, weights,
                                       ALU.is_gt, ALU.mult).then_inc(hits_done, 1)
                v.tensor_scalar(marks[:, T, :], y[:, T, 0:3], HALF, None, ALU.is_gt).then_inc(marks_done, 1)
                v.tensor_copy(feat[:, T, 4:8:2], y[:, T, X_OP:X_OP + 2]).then_inc(op_hi_done, 1)
                dve.wait_ge(marks_done, n)
                v.tensor_tensor(both[:, T, :], marks[:, T, 1:3], marks[:, T, 0:1].to_broadcast([P, nt, 2]), ALU.mult
                                ).then_inc(both_done, 1)
                dve.wait_ge(hits_done, n)
                v.reduce_max(hit_max[:, T, :], first_hit[:, T, :, :], axis=AX.X).then_inc(max_done, 1)
                dve.wait_ge(both_done, n)
                v.tensor_copy(masks[:, par, T, 0], both[:, T, 0])
                v.tensor_tensor(masks[:, par, T, 1], both[:, T, 1], both[:, T, 0], ALU.is_gt).then_inc(masks_done, 1)
                dve.wait_ge(max_done, n)
                v.tensor_scalar(hit_pos[:, T, :], hit_max[:, T, :], -1.0, float(NIB), ALU.mult, ALU.add
                                ).then_inc(pos_done, 1)
                dve.wait_ge(op_hi_done, n)
                v.tensor_tensor(feat[:, T, 5:8:2], y[:, T, X_OP:X_OP + 2], feat[:, T, 4:8:2].bitcast(F32), ALU.subtract)
                dve.wait_ge(pos_done, n)
                v.scalar_tensor_tensor(feat[:, T, 0:4], hit_max[:, T, :], 0.0, hit_pos[:, T, :], ALU.is_gt, ALU.mult
                                       ).then_inc(feat_done, 1)
                dve.wait_ge(masks_done, n)
                v.tensor_tensor(active[:, par, T], masks[:, par, T, 0], masks[:, par, T, 1], ALU.add)
                dve.wait_ge(feat_done, n)
                after(dve, featT_ready, g)
                for m in range(2):
                    ins = v.tensor_tensor(
                        feat_rows[:, T, m * KF // 2:(m + 1) * KF // 2].rearrange("p c (d f) -> p c d f", d=2),
                        feat[:, T, :].bitcast(F32).unsqueeze(2).to_broadcast([P, nt, 2, NFEAT]),
                        masks[:, par, T, m:m + 1].unsqueeze(3).to_broadcast([P, nt, 2, NFEAT]), ALU.mult)
                ins.then_inc(rows_ready, 1)

            def back(s, par, nt):
                n, T = s + 1, slice(0, nt)
                dve.wait_ge(y3_ready, n)
                v.tensor_tensor(y3[:, T, :], ps_y[:, T, :], b3[:, :].unsqueeze(1).to_broadcast([P, nt, 6]), ALU.add
                                ).then_inc(y3_read, 1)
                dve.wait_ge(y3_read, n)
                v.tensor_tensor(y3m[:, T, :].rearrange("p c (o m) -> p c o m", m=2),
                                y3[:, T, :].rearrange("p c (o m) -> p c o m", m=2),
                                masks[:, par, T, :].unsqueeze(2).to_broadcast([P, nt, 3, 2]), ALU.mult).then_inc(p3[0], 1)
                dve.wait_ge(p3[0], n)
                v.tensor_tensor(res[:, T, :], y3m[:, T, 0:6:2], y3m[:, T, 1:6:2], ALU.add).then_inc(p3[1], 1)
                dve.wait_ge(p3[1], n)
                v.tensor_scalar(res_c[:, T, :], res[:, T, 0:2], 0.0, float(NIB - 1), ALU.max, ALU.min).then_inc(p3[2], 1)
                v.tensor_scalar(carry_out[:, T], res[:, T, 2], HALF, None, ALU.is_gt)
                dve.wait_ge(p3[2], n)
                v.tensor_scalar(res_up[:, T, :], res_c[:, T, :], MAGIC, None, ALU.add).then_inc(p3[3], 1)
                dve.wait_ge(p3[3], n)
                v.tensor_scalar(res_int[:, T, :], res_up[:, T, :], -MAGIC, None, ALU.add).then_inc(p3[4], 1)
                dve.wait_ge(p3[4], n)
                v.tensor_tensor(is_hot[:, T, :, :],
                                hot[:, :].unsqueeze(1).unsqueeze(1).to_broadcast([P, nt, 2, NIB]),
                                res_int[:, T, :].unsqueeze(3).to_broadcast([P, nt, 2, NIB]), ALU.is_equal).then_inc(p3[5], 1)
                dve.wait_ge(p3[5], n)
                v.scalar_tensor_tensor(is_hot2[:, T, :, :].rearrange("p c o k -> p c (o k)"),
                                       is_hot[:, T, :, :].rearrange("p c o k -> p c (o k)"), 2.0,
                                       active[:, par, T].unsqueeze(2).to_broadcast([P, nt, 2 * NIB]),
                                       ALU.mult, ALU.mult).then_inc(p3[6], 1)
                dve.wait_ge(p3[6], n)
                dve.wait_ge(o_scaled, n)
                lo = o_sb[:, par, T, OUT_LO:CARRY]
                v.tensor_tensor(lo, lo, is_hot2[:, T, :, :].rearrange("p c o k -> p c (o k)"), ALU.add)
                hi = o_sb[:, par, T, CARRY]
                v.tensor_tensor(hi, hi, carry_out[:, T], ALU.add).then_inc(o_done, 1)

            def step(s, par, early=True, mid=True):
                mid_tile, early_tile = TPG * par, TPG * (1 - par)
                if mid:
                    mid_h(s + 1, 1 - par, mid_tile)
                    mid_f(s + 1, 1 - par, TPG, False)
                if early:
                    early_a(s + 2, par, early_tile)
                    early_b(s + 2, par, early_tile)
                back(s, par, 1 if isinstance(s, int) and s == 0 else TPG)

            early_a(1, 1, 0)
            early_b(1, 1, 0)
            mid_f(0, 0, 1, True)
            step(0, 0)
            step(1, 1)
            step(2, 0)
            with dve.Fori(1, BATCH - 1) as b:
                step(2 * b + 1, 1)
                step(2 * b + 2, 0)
            step(GROUPS - 1, 1, early=False)
            step(GROUPS, 0, early=False, mid=False)

        @block.tensor
        def _(pe_):
            t = nc.tensor
            tile = lambda c: slice(c * P, (c + 1) * P)
            count = [0]

            def su(ins):
                count[0] += 1
                ins.then_inc(su_t, 1)

            pe_.wait_ge(const_step, CONSTS)
            pe_.wait_ge(su_v, SU_CENTRED)
            for c in range(DC):
                t.transpose(bank[0][:, tile(c)], B_sb[:, tile(c)], ident[:, :])
            for c in range(DC):
                ins = t.transpose(bank[1][:, tile(c)], W4c[:, tile(c)], ident[:, :])
            su(ins)
            assert count[0] == TS_W
            pe_.wait_ge(ld_c, 16)
            for c in range(DC):
                ins = t.transpose(bank[3][:, tile(c)], C_sb[:, c, :], ident[:, :])
            su(ins)
            assert count[0] == TS_C
            pe_.wait_ge(su_v, SU_BW)
            for c in range(DC):
                ins = t.matmul(bank[2][:, 0:RG], W4T[:, c, :], BW[:, c, :], start=(c == 0), stop=(c == DC - 1))
            su(ins)
            assert count[0] == TS_R
            for c in range(DC):
                ins = t.transpose(bank[0][:, tile(c)], cls_n[:, tile(c)], ident[:, :])
            su(ins)
            assert count[0] == TS_CLST == TS_PE
            for k in range(TILES):
                if k >= 2:
                    pe_.wait_ge(su_a, 6 + k - 1)
                for c in range(DC):
                    ins = t.transpose(bank[4 + k % 2][:, tile(c)], pe_sb[:, k, tile(c)], ident[:, :])
                su(ins)
                pe_.wait_ge(su_a, 6 + k + 1)
                if k >= 2:
                    pe_.wait_ge(su_v, SU_CLST + k - 1)
                for c in range(DC):
                    ins = t.matmul(bank[6 + k % 2][:, 0:RG], peT[:, k % 2, tile(c)], BW[:, c, :],
                                   start=(c == 0), stop=(c == DC - 1))
                su(ins)
            pe_.wait_ge(su_v, SU_CLST)
            for c in range(DC):
                ins = t.matmul(bank[1][:, 0:P], BW[:, c, 0:NS], clsT[:, tile(c)], start=(c == 0), stop=(c == DC - 1))
            su(ins)
            assert count[0] == TS_CLSU
            pe_.wait_ge(ld_f1, 16 * 8)
            pe_.wait_ge(spread_done, 6)
            for m in range(2):
                t.transpose(bank[3][:, tile(m)], top1[:, m, 0:P], ident[:, :])
                t.transpose(bank[3][:, 256 + REM * m:256 + REM * (m + 1)], bot1[:, m, 0:P], ident[0:REM, 0:REM])
                t.transpose(bank[4][:, tile(m)], spread1[:, m, :], ident[:, :])
            t.transpose(bank[5][:, 0:P], diag1[:, :], ident[:, :])
            pe_.wait_ge(su_v, SU_PE)
            for k in range(8):
                ins = t.transpose(bank[6 + k // 4][0:KF, tile(k % 4)],
                                  zr[:, k, :, :, :].rearrange("p m d f -> p (m d f)").bitcast(F32), ident[:, :])
            su(ins)
            assert count[0] == TS_FFN
            pe_.wait_ge(su_v, SU_CLSU)
            su(t.matmul(bank[2][:, :], stateT_cls[:, :], CT[:, :], start=True, stop=True))
            assert count[0] == TS_CLSH
            pe_.wait_ge(su_v, SU_ALL)
            pe_.wait_ge(ld_f3, 16 * 18)

            def early_x(g, par):
                pe_.wait_ge(x_split, g)
                after(pe_, featT_copied, g - 1)
                for c in range(TPG):
                    ins = t.transpose(ps_T[:, tile(c)], x_parts[:, par, c, :, :].rearrange("p n k -> p (n k)").bitcast(F32),
                                      ident[:, :])
                ins.then_inc(xT_ready, 1)

            def early_u(g, par):
                pe_.wait_ge(xT_copied, g)
                after(pe_, y3_read, g - 2)
                for c in range(TPG):
                    ins = t.matmul(ps_var[:, c, :], xT[:, par, tile(c)], r_x[:, NS:RG], start=True, stop=True)
                ins.then_inc(var_ready, 1)
                after(pe_, state_read, g - 1)
                for c in range(TPG):
                    ins = t.matmul(state_v[:, c, :], xT[:, par, tile(c)], r_x[:, 0:NS], start=True, stop=True)
                ins.then_inc(state_ready, 1)

            def early_s(g):
                pe_.wait_ge(state_scaled, g)
                after(pe_, stateT_ready, g - 1)
                for c in range(TPG):
                    ins = t.matmul(ps_scan[:, tile(c)], state_in[:, c, :], tri[:, :], start=True, stop=True)
                ins.then_inc(scan_ready, 1)

            def mid_h(g, par, c):
                if c == 0:
                    pe_.wait_ge(stateT_ready, g)
                if c >= 2:
                    pe_.wait_ge(h_added[c - 2], g)
                else:
                    after(pe_, h_added[c + 2], g - 1)
                t.matmul(ps_h[c % 2][:, :], xT[:, par, tile(c)], w_x[:, :], start=True, stop=False)
                t.matmul(ps_h[c % 2][:, :], stateT[:, par, tile(c)], CT[:, :], start=False, stop=True
                         ).then_inc(h_ready[c], 1)

            def back_f(s, nt):
                pe_.wait_ge(rows_ready, s + 1)
                after(pe_, xT_copied, min(s + 1, GROUPS) if isinstance(s, int) else s + 1)
                for c in range(nt):
                    ins = t.transpose(ps_T[:, tile(c)], feat_rows[:, c, :].bitcast(F32),
                                      ident[:, :])
                ins.then_inc(featT_ready, 1)

            def bank_free(s, k):
                if k >= 2:
                    pe_.wait_ge(f_relu[k - 2], s + 1)
                else:
                    after(pe_, f_relu[k + 6], s)

            def back_1(s, k, n):
                if k == 0:
                    pe_.wait_ge(featT_copied, s + 1)
                bank_free(s, k)
                t.matmul(ps_f[k % 2][:, 0:n], w_feat[:, k, :], featT[:, 0:n], start=True, stop=True).then_inc(f_ready[k], 1)

            def back_2(s, q, n):
                k = 5 + q
                bank_free(s, k)
                o = ps_f[k % 2][:, 0:n]
                t.matmul(o, w_feat[:, k, :], featT[:, 0:n], start=True, stop=False)
                for m in range(2):
                    t.matmul(o, w2_main[:, m, :], hid1[:, 2 * q + m, 0:n], start=False, stop=False)
                pe_.wait_ge(f_relu[4], s + 1)
                t.matmul(o, w2_rem_main[:, q, :], hid1[:, 4, 0:n], start=False, stop=True).then_inc(f_ready[k], 1)

            def back_2r(s, n):
                bank_free(s, 7)
                o = ps_f[1][:, 0:n]
                t.matmul(o, w_feat[:, 7, :], featT[:, 0:n], start=True, stop=False)
                for k in range(4):
                    t.matmul(ps_f[1][REM * k:REM * (k + 1), 0:n], w2_main_rem[:, k % 2, :], hid1[:, k, 0:n],
                             start=False, stop=False)
                t.matmul(o, w2_rem[:, :], hid1[:, 4, 0:n], start=False, stop=True).then_inc(f_ready[7], 1)

            def back_3(s, nt, early_g):
                pe_.wait_ge(f_relu[7], s + 1)
                after(pe_, y3_read, s)
                after(pe_, var_read, early_g)
                for c in range(nt):
                    for k in range(3):
                        ins = t.matmul(ps_y[:, c, :], hid2[:, k, tile(c)], w3[:, k, :], start=(k == 0), stop=(k == 2))
                ins.then_inc(y3_ready, 1)

            def step(s, par, early=True, mid=True):
                cls = isinstance(s, int) and s == 0
                nt, n = (1, P) if cls else (TPG, GT)
                back_f(s, nt)
                back_1(s, 0, n)
                for c in range(TPG):
                    back_1(s, c + 1, n)
                    if mid:
                        mid_h(s + 1, 1 - par, c)
                if early:
                    early_x(s + 2, par)
                back_2(s, 0, n)
                if early:
                    early_u(s + 2, par)
                back_2(s, 1, n)
                back_2r(s, n)
                if early:
                    early_s(s + 2)
                back_3(s, nt, s + 2 if early else GROUPS)

            early_x(1, 1)
            early_u(1, 1)
            early_s(1)
            step(0, 0)
            step(1, 1)
            step(2, 0)
            with pe_.Fori(1, BATCH - 1) as b:
                step(2 * b + 1, 1)
                step(2 * b + 2, 0)
            step(GROUPS - 1, 1, early=False)
            step(GROUPS, 0, early=False, mid=False)


_INS = ["x", "cls_tok", "L0_tok_W", "L0_attn_log_lambda", "L0_attn_B", "L0_attn_C", "L0_attn_log_dt",
        "L0_ffn_Wa", "L0_ffn_ba", "L0_ffn_Ws", "L0_ffn_bs"]


def kernel(**inputs):
    import concourse.bacc as bacc
    from concourse.bass_utils import run_bass_kernel_spmd

    nc = bacc.Bacc("TRN2", target_bir_lowering=False, num_devices=1)
    arrays, args = {}, []

    def give(name, a):
        arrays[name] = a
        args.append(nc.dram_tensor(name, a.shape, mybir.dt.from_np(a.dtype), kind="ExternalInput").ap())

    for name in _INS:
        a = np.ascontiguousarray(inputs[name])
        give(f"in_{name}", a.reshape(1) if a.ndim == 0 else a)
    batch, height, width, _ = arrays["in_x"].shape
    d_model = arrays["in_L0_tok_W"].shape[1]
    give("pe", position_table(height * width, d_model))
    out = nc.dram_tensor("out", (batch, height * width + 1, d_model), F32, kind="ExternalOutput").ap()
    vit_layer(nc, *args, out)
    r = run_bass_kernel_spmd(nc, [arrays], core_ids=[0])
    return r.results[0]["out"]
```

```python
import math
from contextlib import ExitStack

import numpy as np
import concourse.bass as bass
from concourse import mybir

F32 = mybir.dt.float32
F32R = mybir.dt.float32r
ALU = mybir.AluOpType
ACT = mybir.ActivationFunctionType
AX = mybir.AxisListType


def position_table(seq_len, d_model):
    position = np.arange(seq_len, dtype=np.float32)[:, None]
    div_term = np.exp(np.arange(0, d_model, 2, dtype=np.float32) * (-math.log(10000.0) / d_model))
    pe = np.zeros((seq_len, d_model), dtype=np.float32)
    pe[:, 0::2] = np.sin(position * div_term)
    pe[:, 1::2] = np.cos(position * div_term)
    return pe


def after(eng, sem, count):
    if isinstance(count, int) and count <= 0:
        return
    eng.wait_ge(sem, count)


SU_CENTRED, SU_BW, SU_CLSVE, SU_CLSN, SU_PARTS, SU_PE, SU_VAR, SU_CLST, SU_FFN, SU_CLSU, SU_ALL = (
    6, 7, 10, 15, 19, 27, 28, 29, 30, 31, 32)
TS_W, TS_C, TS_R, TS_PE, TS_CLST, TS_FFN, TS_CLSU, TS_CLSH = 1, 2, 3, 3, 12, 13, 14, 15
SA_ROOT, SA_C, SA_EXP, SA_FFN = 3, 4, 10, 17
IDENT, CONSTS = 4, 17


def pe_copied(k):
    return SA_C + 1 + k if k < 4 else SA_EXP + 1 + k - 4


def vit_layer(nc, x, cls_tok, tok_w, log_lambda, B, C, log_dt, Wa, ba, Ws, bs, pe, out):
    P = 128
    BATCH, GRID_H, GRID_W, F = x.shape
    D = tok_w.shape[1]
    NS = B.shape[0]
    TOK = GRID_H * GRID_W
    TPG = 4
    GT = TPG * P
    TILES = TOK // P
    GROUPS = BATCH * TOK // GT
    DC = D // P
    BLK = 32
    NB = P // BLK
    RG = NS + BLK
    GE = Wa.shape[1]
    REM = GE - P
    EPS = 1e-5
    HALF = 0.5
    NIB_A, OPC_ADD, ALU_LO, OP_START = 0, 25, 16, 10
    IN_OP = OP_START + OPC_ADD
    X_OP = 80 + OPC_ADD
    FIELDS, NIB = 4, 16
    YC = X_OP + 2
    RESULT = 100
    OUT_LO, CARRY = 128, 160
    NFEAT = 9
    KF = 2 * 2 * NFEAT
    MAGIC = 1.5 * 2.0 ** 23
    assert D == 512 and NS == P and F <= BLK - 1 and TILES == 2 * TPG and REM == 32

    xf = x.rearrange("b h w f -> (b h w) f")
    pipes = ((Wa, ba), (Ws, bs))

    ctx = ExitStack()
    with ctx:
        def sb(name, shape, dt=F32):
            return ctx.enter_context(nc.sbuf_tensor(name, shape, dt))

        def sem(name):
            return ctx.enter_context(nc.semaphore(name))

        ident = sb("ident", [P, P])
        tri = sb("tri", [P, P])
        pe_sb = sb("pe_sb", [P, TILES, D])
        pe_state = sb("pe_state", [P, TILES, NS])
        pe_var = sb("pe_var", [P, TILES, BLK])
        var_pe = sb("var_pe", [P, TILES, 2])
        decayT = sb("decayT", [P, TOK])
        inv_decay = sb("inv_decay", [P, TILES, NS])
        w_x = sb("w_x", [P, D], F32R)
        r_x = sb("r_x", [P, RG], F32R)
        CT = sb("CT", [P, D])
        w_feat = sb("w_feat", [KF, 8, P], F32R)
        w2_main = sb("w2_main", [P, 2, P])
        w2_main_rem = sb("w2_main_rem", [P, 2, REM])
        w2_rem_main = sb("w2_rem_main", [P, 2, P])
        w2_rem = sb("w2_rem", [P, P])
        w3 = sb("w3", [P, 3, REM])
        b3 = sb("b3", [3 * REM, 1])
        pick3 = sb("pick3", [3 * REM, 6])
        nib_w = sb("nib_w", [P, FIELDS, NIB])
        hot = sb("hot", [P, NIB])
        ones4 = sb("ones4", [P, TPG])
        carry_cls = sb("carry_cls", [P, 1])
        B_sb = sb("B_sb", [P, D])
        C_sb = sb("C_sb", [P, DC, P])
        W4 = sb("W4", [P, D])
        W4c = sb("W4c", [P, D])
        w_hi = sb("w_hi", [P, D], F32R)
        r_all = sb("r_all", [P, RG])
        r_hi = sb("r_hi", [P, RG], F32R)
        BW = sb("BW", [P, DC, RG])
        W4T = sb("W4T", [P, DC, P])
        peT = sb("peT", [P, 2, D])
        mean_b = sb("mean_b", [P, 1])
        mean_w = sb("mean_w", [P, 1])
        stat_pe = sb("stat_pe", [P, TILES, 6])
        ll_col = sb("ll_col", [P, 2])
        ll_row = sb("ll_row", [P, NS])
        ld_col = sb("ld_col", [P, 1])
        ld_row = sb("ld_row", [P, NS])
        t_row = sb("t_row", [P, TOK])
        t_col = sb("t_col", [P, TILES])
        top1 = sb("top1", [P, 2, GE])
        bot1 = sb("bot1", [REM, 2, GE])
        diag1 = sb("diag1", [P, P])
        spread1 = sb("spread1", [P, 2, P])
        top0 = sb("top0", [P, 2, GE])
        rem0 = sb("rem0", [P, GE])
        bias_main = sb("bias_main", [P, 2, 2])
        bias_rem = sb("bias_rem", [P, 2])
        zf = sb("zf", [P, 8, 2, NFEAT])
        zr = sb("zr", [P, 8, 2, 2, NFEAT], F32R)
        cls_sb = sb("cls_sb", [P, D])
        cls_st = sb("cls_st", [P, 6])
        cls_mv = sb("cls_mv", [P, 2])
        cls_ve = sb("cls_ve", [P, 1])
        cls_sd = sb("cls_sd", [P, 1])
        cls_r = sb("cls_r", [P, 4])
        cls_n = sb("cls_n", [P, D])
        clsT = sb("clsT", [P, D])
        stateT_cls = sb("stateT_cls", [P, P])
        x_in = sb("x_in", [P, 2, TPG, F])
        x_parts = sb("x_parts", [P, 2, TPG, NB, BLK], F32R)
        xT = sb("xT", [P, 2, GT], F32R)
        q_prod = sb("q_prod", [P, TPG, F])
        q_sum = sb("q_sum", [P, TPG])
        ve1 = sb("ve1", [P, TPG])
        sd1 = sb("sd1", [P, TPG])
        rs1 = sb("rs1", [P, 4, TPG])
        state_raw = sb("state_raw", [P, TPG, NS])
        state_in = sb("state_in", [P, TPG, NS])
        carry = sb("carry", [P, 2, TPG])
        stateT = sb("stateT", [P, 2, GT])
        h1 = sb("h1", [P, 2, TPG, D])
        st2 = sb("st2", [P, TPG, 6])
        mv2 = sb("mv2", [P, TPG, 2])
        ve2 = sb("ve2", [P, TPG])
        sd2 = sb("sd2", [P, TPG])
        rs2 = sb("rs2", [P, 4, TPG])
        out_scale = sb("out_scale", [P, 2, TPG])
        out_bias = sb("out_bias", [P, 2, TPG])
        y = sb("y", [P, TPG, YC])
        first_hit = sb("first_hit", [P, TPG, FIELDS, NIB])
        hit_max = sb("hit_max", [P, TPG, FIELDS])
        hit_pos = sb("hit_pos", [P, TPG, FIELDS])
        marks = sb("marks", [P, TPG, 3])
        both = sb("both", [P, TPG, 2])
        masks = sb("masks", [P, 2, TPG, 2])
        active = sb("active", [P, 2, TPG])
        feat = sb("feat", [P, TPG, NFEAT], F32R)
        feat_rows = sb("feat_rows", [P, TPG, P], F32R)
        featT = sb("featT", [KF, GT], F32R)
        hid1 = sb("hid1", [P, 5, GT])
        hid2 = sb("hid2", [P, 3, GT])
        y3T = sb("y3T", [3 * REM, GT])
        y3m = sb("y3m", [P, TPG, 6])
        res = sb("res", [P, TPG, 3])
        res_c = sb("res_c", [P, TPG, 2])
        res_up = sb("res_up", [P, TPG, 2])
        res_int = sb("res_int", [P, TPG, 2])
        is_hot = sb("is_hot", [P, TPG, 2, NIB])
        is_hot2 = sb("is_hot2", [P, TPG, 2, NIB])
        carry_out = sb("carry_out", [P, TPG])
        o_sb = sb("o_sb", [P, 2, TPG, D])

        bank = [ctx.enter_context(nc.psum_tensor(f"bank{n}", [P, 512], F32)) for n in range(8)]
        ps_T, ps_small, ps_state, ps_scan = bank[0], bank[1], bank[2], bank[3]
        ps_h, ps_f = bank[4:6], bank[6:8]
        u3 = ps_state[:, 0:3 * RG].rearrange("p (c k) -> p c k", c=3)
        u1 = ps_small[:, 0:RG].unsqueeze(1)
        ps_y = ps_small[:, 0:TPG * 6].rearrange("p (c k) -> p c k", c=TPG)

        ld_b, ld_w, ld_c, ld_lam, ld_cls = (sem(n) for n in ("ld_b", "ld_w", "ld_c", "ld_lam", "ld_cls"))
        ld_pe = [sem(f"ld_pe{n}") for n in range(TILES // 2)]
        ld_f1, ld_f0, ld_f3 = sem("ld_f1"), sem("ld_f0"), sem("ld_f3")
        zeroed = sem("zeroed")
        const_step = sem("const_step")
        su_v = sem("su_v")
        su_a = sem("su_a")
        su_tp = sem("su_tp")
        su_t = sem("su_t")
        clip_step = sem("clip_step")
        decay_ready = sem("decay_ready")
        spread_done = sem("spread_done")
        x_loaded = [sem("x_loaded0"), sem("x_loaded1")]
        x_hi = sem("x_hi")
        x_split, xT_ready, xT_copied = sem("x_split"), sem("xT_ready"), sem("xT_copied")
        u_ready, var_read, state_read = sem("u_ready"), sem("var_read"), sem("state_read")
        v1 = [sem(f"v1_{n}") for n in range(8)]
        sd1_ready = sem("sd1_ready")
        state_scaled, scan_ready, carry_ready, stateT_ready = sem("state_scaled"), sem("scan_ready"), sem("carry_ready"), sem("stateT_ready")
        h_ready = [sem(f"h_ready{c}") for c in range(TPG)]
        h_added = [sem(f"h_added{c}") for c in range(TPG)]
        h_stat, h_aggr = sem("h_stat"), sem("h_aggr")
        v2 = [sem(f"v2_{n}") for n in range(5)]
        ve2_ready, sd2_ready, scale_ready = sem("ve2_ready"), sem("sd2_ready"), sem("scale_ready")
        y_done, hits_done, max_done, pos_done, op_hi_done, marks_done, both_done, masks_done, feat_done = (
            sem(n) for n in ("y_done", "hits_done", "max_done", "pos_done", "op_hi_done", "marks_done",
                             "both_done", "masks_done", "feat_done"))
        rows_ready, featT_ready, featT_copied = sem("rows_ready"), sem("featT_ready"), sem("featT_copied")
        f_ready = [sem(f"f_ready{k}") for k in range(8)]
        f_relu = [sem(f"f_relu{k}") for k in range(8)]
        y3_parts, y3_copied, y3_ready = sem("y3_parts"), sem("y3_copied"), sem("y3_ready")
        p3 = [sem(f"p3_{n}") for n in range(8)]
        o_scaled, o_done = sem("o_scaled"), sem("o_done")
        o_stored = [sem("o_stored0"), sem("o_stored1")]

        block = ctx.enter_context(nc.Block())

        def load_x(eng, g, row, par):
            after(eng, x_split, g - 2)
            after(eng, v1[1], g - 2)
            eng.dma_start(x_in[:, par, :, :], xf[bass.ds(row, GT), :].rearrange("(c p) f -> p c f", p=P)
                          ).then_inc(x_loaded[par], 16)

        def store(eng, g, b, half, par):
            after(eng, o_done, g + 1)
            eng.dma_start(out[b, 1 + half * GT:1 + (half + 1) * GT, :].rearrange("(c p) d -> p c d", p=P),
                          o_sb[:, par, :, :]).then_inc(o_stored[par], 16)

        @block.sync
        def _(sp):
            sp.dma_start(B_sb[:, :], B).then_inc(ld_b, 16)
            sp.wait_ge(zeroed, 1)
            for n in range(NB):
                sp.dma_start(W4[n * BLK:n * BLK + F, :], tok_w).then_inc(ld_w, 16)
            for c in range(0, TILES, 2):
                sp.dma_start(pe_sb[:, c:c + 2, :], pe[c * P:(c + 2) * P, :].rearrange("(c p) d -> p c d", p=P)
                             ).then_inc(ld_pe[c // 2], 16)
            sp.dma_start(cls_sb[:, :], cls_tok[0, :, :].to_broadcast([P, D])).then_inc(ld_cls, 16)
            load_x(sp, 1, 0, 1)
            load_x(sp, 2, GT, 0)
            sp.wait_ge(zeroed, 4)
            for m, (w, bb) in enumerate(pipes):
                sp.dma_start(top1[:, m, :], w[1, 0:P, :]).then_inc(ld_f1, 16)
                sp.dma_start(bot1[:, m, :], w[1, P:GE, :]).then_inc(ld_f1, 16)
                sp.dma_start(top0[:, m, :], w[0, 0:P, :]).then_inc(ld_f0, 16)
                sp.dma_start(bias_main[:, :, m:m + 1], bb[0:2, 0:P].rearrange("l (p o) -> p l o", o=1),
                             allow_slow_non_contiguous=True).then_inc(ld_f0, 16)
            for q in range(2):
                for m, (w, bb) in enumerate(pipes):
                    r = slice(REM * (2 * q + m), REM * (2 * q + m + 1))
                    sp.dma_start(diag1[r, r], w[1, P:GE, P:GE]).then_inc(ld_f1, 16)
                    sp.dma_start(rem0[r, :], w[0, P:GE, :]).then_inc(ld_f0, 16)
                    sp.dma_start(bias_rem[r, :].unsqueeze(2), bb[0:2, P:GE].rearrange("l (p o) -> p l o", o=1),
                                 allow_slow_non_contiguous=True).then_inc(ld_f0, 16)
            for m, (w, bb) in enumerate(pipes):
                for o, row, q in ((0, RESULT, 0), (1, RESULT, 1), (2, RESULT + 1, 1)):
                    col = 2 * o + m
                    r = slice(REM * (2 * q + m), REM * (2 * q + m + 1))
                    sp.dma_start(w3[:, q, col:col + 1], w[2, row, 0:P].unsqueeze(1),
                                 allow_slow_non_contiguous=True).then_inc(ld_f3, 16)
                    sp.dma_start(w3[r, 2, col:col + 1], w[2, row, P:GE].unsqueeze(1),
                                 allow_slow_non_contiguous=True).then_inc(ld_f3, 16)
                    sp.dma_start(b3[col:col + 1, :], bb[2, row:row + 1].unsqueeze(0)).then_inc(ld_f3, 16)
            load_x(sp, 3, 2 * GT, 1)
            sp.wait_ge(o_done, 1)
            sp.dma_start(out[:, 0, :], o_sb[0:BATCH, 0, 0, :]).then_inc(o_stored[0], 16)
            load_x(sp, 4, 3 * GT, 0)
            store(sp, 1, 0, 0, 1)
            load_x(sp, 5, 4 * GT, 1)
            store(sp, 2, 0, 1, 0)
            with sp.Fori(1, BATCH - 2) as b:
                for half in range(2):
                    load_x(sp, 2 * b + 4 + half, (2 * b + 3 + half) * GT, half)
                    store(sp, 2 * b + 1 + half, b, half, 1 - half)
            load_x(sp, GROUPS, (GROUPS - 1) * GT, 0)
            store(sp, GROUPS - 3, BATCH - 2, 0, 1)
            store(sp, GROUPS - 2, BATCH - 2, 1, 0)
            store(sp, GROUPS - 1, BATCH - 1, 0, 1)
            store(sp, GROUPS, BATCH - 1, 1, 0)
            sp.wait_ge(o_stored[1], 16 * BATCH)
            sp.wait_ge(o_stored[0], 16 * (BATCH + 1))

        @block.gpsimd
        def _(pool):
            g = nc.gpsimd
            g.memset(W4[:, :], 0.0).then_inc(zeroed, 1)
            g.memset(ident[:, :], 0.0).then_inc(const_step, 1)
            g.memset(tri[:, :], 1.0).then_inc(const_step, 1)
            g.memset(diag1[:, :], 0.0).then_inc(zeroed, 1)
            g.memset(w3[:, :, :], 0.0).then_inc(zeroed, 1)
            g.memset(b3[:, :], 0.0).then_inc(zeroed, 1)
            pool.wait_ge(const_step, 2)
            g.affine_select(out=ident[:, :], in_=ident[:, :], compare_op=ALU.not_equal, fill=1.0, base=0,
                            pattern=[[-1, P]], channel_multiplier=1).then_inc(const_step, 1)
            g.affine_select(out=tri[:, :], in_=tri[:, :], compare_op=ALU.is_ge, fill=0.0, base=0,
                            pattern=[[1, P]], channel_multiplier=-1).then_inc(const_step, 1)
            imp = dict(allow_small_or_imprecise_dtypes=True)
            g.iota(t_row[:, :], pattern=[[1, TOK]], base=1, channel_multiplier=0, **imp).then_inc(const_step, 1)
            g.iota(t_col[:, :], pattern=[[P, TILES]], base=1, channel_multiplier=1, **imp).then_inc(const_step, 1)
            g.iota(nib_w[:, :, :], pattern=[[0, FIELDS], [-1, NIB]], base=NIB, channel_multiplier=0, **imp).then_inc(const_step, 1)
            g.iota(hot[:, :], pattern=[[1, NIB]], base=0, channel_multiplier=0, **imp).then_inc(const_step, 1)
            g.memset(x_parts[:, :, :, :, :].bitcast(F32), 0.0).then_inc(const_step, 1)
            g.memset(zf[:, :, :, :], 0.0).then_inc(const_step, 1)
            g.memset(spread1[:, :, :], 0.0).then_inc(const_step, 1)
            g.memset(ones4[:, :], 1.0).then_inc(const_step, 1)
            g.memset(feat_rows[:, :, :].bitcast(F32), 0.0).then_inc(const_step, 1)
            g.memset(pick3[:, :], 0.0).then_inc(const_step, 1)
            for k in range(3):
                pool.wait_ge(const_step, CONSTS - 3 + k)
                g.affine_select(out=pick3[:, :], in_=pick3[:, :], compare_op=ALU.not_equal, fill=1.0, base=-REM * k,
                                pattern=[[-1, 6]], channel_multiplier=1).then_inc(const_step, 1)
            pool.wait_ge(const_step, CONSTS)

            def split_x(n, par):
                after(pool, x_loaded[par], 16 * n["load"])
                after(pool, xT_ready, n["g"] - 2)
                parts, xin = x_parts[:, par, :, :, :], x_in[:, par, :, :]
                g.tensor_tensor(parts[:, :, 0, 0:F], xin, ones4[:, :].unsqueeze(2).to_broadcast([P, TPG, F]), ALU.mult).then_inc(x_hi, 1)
                g.tensor_copy(parts[:, :, 2, 0:F], xin).then_inc(x_hi, 1)
                after(pool, x_hi, 2 * n["g"])
                g.tensor_tensor(parts[:, :, 1, 0:F], xin, parts[:, :, 0, 0:F].bitcast(F32), ALU.subtract)
                g.tensor_tensor(parts[:, :, 3, 0:F], xin, parts[:, :, 0, 0:F].bitcast(F32), ALU.subtract
                                ).then_inc(x_split, 1)

            pool.wait_ge(su_a, 2)
            g.tensor_scalar(ld_col[:, :], ll_col[:, 0:1], ll_col[:, 1:2], -1.0, ALU.mult, ALU.mult).then_inc(clip_step, 1)
            g.tensor_scalar(ld_row[:, :], ll_row[:, :], ll_col[:, 1:2], -1.0, ALU.mult, ALU.mult).then_inc(clip_step, 1)
            pool.wait_ge(clip_step, 2)
            for c in range(TILES):
                g.tensor_scalar(inv_decay[:, c, :], ld_row[:, :], t_col[:, c:c + 1], -30.0, ALU.mult, ALU.max
                                ).then_inc(clip_step, 1)
            g.tensor_scalar(decayT[:, :], t_row[:, :], ld_col[:, 0:1], -30.0, ALU.mult, ALU.max).then_inc(clip_step, 1)
            pool.wait_ge(clip_step, 3 + TILES)
            g.tensor_scalar(inv_decay[:, :, :], inv_decay[:, :, :], 0.0, None, ALU.min).then_inc(clip_step, 1)
            g.tensor_scalar(decayT[:, :], decayT[:, :], 0.0, None, ALU.min).then_inc(clip_step, 1)
            split_x(dict(g=1, load=1), 1)
            split_x(dict(g=2, load=1), 0)
            pool.wait_ge(su_a, SA_EXP)
            g.tensor_scalar(inv_decay[:, :, :], inv_decay[:, :, :], 1e6, None, ALU.min).then_inc(decay_ready, 1)
            split_x(dict(g=3, load=2), 1)
            split_x(dict(g=4, load=2), 0)
            with pool.Fori(1, BATCH - 1) as b:
                for half in range(2):
                    split_x(dict(g=2 * b + 3 + half, load=b + 2), 1 - half)

        @block.scalar
        def _(act):
            a = nc.scalar
            act.dma_start(ll_col[:, 0:1], log_lambda.unsqueeze(1)).then_inc(ld_lam, 16)
            act.dma_start(ll_row[:, :], log_lambda.unsqueeze(0).to_broadcast([P, NS])).then_inc(ld_lam, 16)
            act.dma_start(ll_col[:, 1:2], log_dt.unsqueeze(0).to_broadcast([P, 1])).then_inc(ld_lam, 16)
            act.dma_start(C_sb[:, :, :], C.rearrange("(c p) n -> p c n", p=P)).then_inc(ld_c, 16)
            act.wait_ge(ld_lam, 48)
            a.activation(ll_col[:, :], ll_col[:, :], ACT.Exp).then_inc(su_a, 1)
            a.activation(ll_row[:, :], ll_row[:, :], ACT.Exp).then_inc(su_a, 1)
            act.wait_ge(su_v, SU_CLSVE)
            a.activation(cls_sd[:, :], cls_ve[:, :], ACT.Sqrt).then_inc(su_a, 1)
            act.wait_ge(su_t, TS_C)
            a.copy(CT[:, :], bank[3][:, :]).then_inc(su_a, 1)
            for c in range(TILES):
                if c == 4:
                    act.wait_ge(clip_step, 5 + TILES)
                    a.activation(decayT[:, :], decayT[:, :], ACT.Exp).then_inc(su_a, 1)
                    a.activation(inv_decay[:, :, :], inv_decay[:, :, :], ACT.Exp, scale=-1.0).then_inc(su_a, 1)
                act.wait_ge(su_tp, c + 1)
                if c >= 2:
                    act.wait_ge(su_t, TS_PE + c - 1)
                a.copy(peT[:, c % 2, :], bank[4 + c % 2][:, :]).then_inc(su_a, 1)
            act.wait_ge(su_t, TS_FFN)
            a.copy(w2_rem_main[:, :, :], bank[4][:, 0:2 * P].rearrange("p (m k) -> p m k", m=2)).then_inc(su_a, 1)
            a.copy(w_feat[:, 0:4, :], bank[6][0:KF, :].rearrange("p (m k) -> p m k", m=4)).then_inc(su_a, 1)
            a.copy(w_feat[:, 4:8, :], bank[7][0:KF, :].rearrange("p (m k) -> p m k", m=4)).then_inc(su_a, 1)

            def copy_featT(s):
                n = P if isinstance(s, int) and s == 0 else GT
                act.wait_ge(featT_ready, s + 1)
                a.copy(featT[:, 0:n], ps_T[0:KF, 0:n]).then_inc(featT_copied, 1)

            def relu(s, k):
                n = P if isinstance(s, int) and s == 0 else GT
                act.wait_ge(f_ready[k], s + 1)
                dst = hid1[:, k, 0:n] if k < 5 else hid2[:, k - 5, 0:n]
                a.activation(dst, ps_f[k % 2][:, 0:n], ACT.Relu, bias=bias_rem[:, 1:2] if k == 7 else 0.0
                             ).then_inc(f_relu[k], 1)

            def copy_y3T(s):
                n = P if isinstance(s, int) and s == 0 else GT
                act.wait_ge(y3_parts, s + 1)
                a.activation(y3T[:, 0:n], ps_small[0:3 * REM, 0:n], ACT.Identity, bias=b3[:, 0:1]).then_inc(y3_copied, 1)

            def copy_xT(g, par):
                act.wait_ge(xT_ready, g)
                after(act, h_ready[TPG - 1], g - 2)
                a.copy(xT[:, par, :], ps_T[:, :]).then_inc(xT_copied, 1)

            def sqrt1(g):
                act.wait_ge(v1[3], g)
                a.activation(sd1[:, :], ve1[:, :], ACT.Sqrt).then_inc(sd1_ready, 1)

            def sqrt2(g, nt):
                act.wait_ge(ve2_ready, g + 1)
                a.activation(sd2[:, 0:nt], ve2[:, 0:nt], ACT.Sqrt).then_inc(sd2_ready, 1)

            def scale_out(s, par, tiles, nstore, last):
                act.wait_ge(scale_ready, s + 1)
                after(act, o_stored[par], 16 * nstore)
                for c in tiles:
                    ins = a.activation(o_sb[:, par, c, :], h1[:, par, c, :], ACT.Identity,
                                       bias=out_bias[:, par, c:c + 1], scale=out_scale[:, par, c:c + 1])
                if last:
                    ins.then_inc(o_scaled, 1)

            def step(s, par, nstore, early=True, mid=True):
                cls = isinstance(s, int) and s == 0
                copy_featT(s)
                relu(s, 0)
                relu(s, 1)
                if early:
                    copy_xT(s + 2, par)
                for k in range(2, 5):
                    relu(s, k)
                scale_out(s, par, range(1 if cls else 2), nstore, cls)
                if early:
                    sqrt1(s + 2)
                if mid:
                    sqrt2(s + 1, TPG)
                relu(s, 5)
                if not cls:
                    scale_out(s, par, range(2, TPG), nstore, True)
                relu(s, 6)
                relu(s, 7)
                copy_y3T(s)

            act.wait_ge(ld_f3, 16 * 18)
            act.wait_ge(ld_f0, 16 * 12)
            copy_xT(1, 1)
            sqrt1(1)
            sqrt2(0, 1)
            step(0, 0, 0)
            step(1, 1, 0)
            step(2, 0, 1)
            with act.Fori(1, BATCH - 1) as b:
                step(2 * b + 1, 1, b)
                step(2 * b + 2, 0, b + 1)
            step(GROUPS - 1, 1, BATCH - 1, early=False)
            step(GROUPS, 0, BATCH, early=False, mid=False)

        @block.vector
        def _(dve):
            v = nc.vector
            done = [0]

            def su(ins):
                done[0] += 1
                ins.then_inc(su_v, 1)
                dve.wait_ge(su_v, done[0])

            dve.wait_ge(ld_b, 16)
            su(v.reduce_sum(mean_b[:, :], B_sb[:, :], axis=AX.X))
            su(v.tensor_scalar(mean_b[:, :], mean_b[:, :], 1.0 / D, None, ALU.mult))
            su(v.tensor_scalar(B_sb[:, :], B_sb[:, :], mean_b[:, 0:1], None, ALU.subtract))
            dve.wait_ge(ld_w, 16 * NB)
            su(v.reduce_sum(mean_w[:, :], W4[:, :], axis=AX.X))
            su(v.tensor_scalar(mean_w[:, :], mean_w[:, :], 1.0 / D, None, ALU.mult))
            su(v.tensor_scalar(W4c[:, :], W4[:, :], mean_w[:, 0:1], None, ALU.subtract))
            assert done[0] == SU_CENTRED
            dve.wait_ge(su_t, TS_W)
            v.tensor_copy(BW[:, :, 0:NS], bank[0][:, :].rearrange("p (c k) -> p c k", c=DC))
            v.tensor_copy(BW[:, :, NS:RG], bank[1][:, :].rearrange("p (c k) -> p c k", c=DC)[:, :, 0:BLK])
            su(v.tensor_copy(W4T[:, :, :], bank[1][:, :].rearrange("p (c k) -> p c k", c=DC)))
            assert done[0] == SU_BW
            dve.wait_ge(ld_cls, 16)
            su(v.bn_stats(cls_st[:, :], cls_sb[:, :]))
            su(v.bn_aggr(cls_mv[:, :], cls_st[:, :]))
            su(v.tensor_scalar(cls_ve[:, :], cls_mv[:, 1:2], EPS, None, ALU.add))
            assert done[0] == SU_CLSVE
            dve.wait_ge(su_a, SA_ROOT)
            su(v.reciprocal(cls_r[:, 0:1], cls_sd[:, :]))
            su(v.tensor_tensor(cls_r[:, 1:2], cls_r[:, 0:1], cls_r[:, 0:1], ALU.mult))
            su(v.scalar_tensor_tensor(cls_r[:, 2:3], cls_r[:, 1:2], -0.5, cls_ve[:, :], ALU.mult, ALU.mult))
            su(v.scalar_tensor_tensor(cls_r[:, 3:4], cls_r[:, 2:3], 1.5, cls_r[:, 0:1], ALU.add, ALU.mult))
            su(v.tensor_scalar(cls_n[:, :], cls_sb[:, :], cls_mv[:, 0:1], cls_r[:, 3:4], ALU.subtract, ALU.mult))
            assert done[0] == SU_CLSN
            v.tensor_copy(w_hi[:, :], W4[:, :])
            su(v.tensor_copy(w_x[0:64, :], W4[0:64, :]))
            v.tensor_tensor(w_x[64:P, :], W4[64:P, :], w_hi[64:P, :].bitcast(F32), ALU.subtract)
            dve.wait_ge(su_t, TS_R)
            su(v.tensor_copy(r_all[:, :], bank[2][:, 0:RG]))
            v.tensor_copy(r_hi[:, :], r_all[:, :])
            su(v.tensor_copy(r_x[0:64, :], r_all[0:64, :]))
            su(v.tensor_tensor(r_x[64:P, :], r_all[64:P, :], r_hi[64:P, :].bitcast(F32), ALU.subtract))
            assert done[0] == SU_PARTS
            for c in range(TILES):
                dve.wait_ge(ld_pe[c // 2], 16)
                v.bn_stats(stat_pe[:, c, :], pe_sb[:, c, :])
                dve.wait_ge(su_t, TS_PE + c + 1)
                v.tensor_copy(pe_state[:, c, :], bank[6 + c % 2][:, 0:NS])
                su(v.tensor_scalar(pe_var[:, c, :], bank[6 + c % 2][:, NS:RG], 2.0, None, ALU.mult))
            assert done[0] == SU_PE
            for c in range(TILES):
                ins = v.bn_aggr(var_pe[:, c, :], stat_pe[:, c, :])
            su(ins)
            assert done[0] == SU_VAR
            dve.wait_ge(su_t, TS_CLST)
            su(v.tensor_copy(clsT[:, :], bank[0][:, :]))
            assert done[0] == SU_CLST
            dve.wait_ge(const_step, CONSTS)
            dve.wait_ge(ld_f1, 16 * 8)
            dve.wait_ge(ld_f0, 16 * 12)
            for q in range(2):
                for m in range(2):
                    k, r = 2 * q + m, slice(REM * (2 * q + m), REM * (2 * q + m + 1))
                    v.tensor_copy(spread1[:, q, REM * k:REM * (k + 1)], top1[:, m, P:GE])
                    v.tensor_copy(zf[:, k, m, q:q + 3:2], top0[:, m, 0:2])
                    v.tensor_copy(zf[:, k, m, 4:8].rearrange("p (o d) -> p o d", d=2),
                                  top0[:, m, IN_OP:IN_OP + 2].unsqueeze(2).to_broadcast([P, 2, 2]))
                    v.tensor_copy(zf[:, k, m, 8:9], bias_main[:, 0, m:m + 1])
                    v.tensor_copy(zf[:, 5 + q, m, 8:9], bias_main[:, 1, m:m + 1])
                    v.tensor_copy(zf[r, 4, m, q:q + 3:2], rem0[r, 0:2])
                    v.tensor_copy(zf[r, 4, m, 4:8].rearrange("p (o d) -> p o d", d=2),
                                  rem0[r, IN_OP:IN_OP + 2].unsqueeze(2).to_broadcast([REM, 2, 2]))
                    v.tensor_copy(zf[r, 4, m, 8:9], bias_rem[r, 0:1])
                    v.tensor_copy(zf[r, 7, m, 8:9], bias_rem[r, 1:2]).then_inc(spread_done, 1)
            dve.wait_ge(spread_done, 4)
            v.tensor_copy(zr[:, :, :, 0, :], zf[:, :, :, :]).then_inc(spread_done, 1)
            dve.wait_ge(spread_done, 5)
            v.tensor_tensor(zr[:, :, :, 1, :], zf[:, :, :, :], zr[:, :, :, 0, :].bitcast(F32),
                            ALU.subtract).then_inc(spread_done, 1)
            dve.wait_ge(su_t, TS_FFN)
            v.tensor_copy(w2_main[:, :, :], bank[5][:, 0:2 * P].rearrange("p (m k) -> p m k", m=2))
            v.tensor_copy(w2_main_rem[:, :, :], bank[5][:, 256:256 + 2 * REM].rearrange("p (m k) -> p m k", m=2))
            su(v.tensor_copy(w2_rem[:, :], bank[5][:, 320:320 + P]))
            assert done[0] == SU_FFN
            dve.wait_ge(su_t, TS_CLSU)
            v.tensor_copy(stateT_cls[:, :], bank[3][:, 0:P])
            su(v.tensor_copy(carry_cls[:, :], bank[3][:, 0:1]))
            assert done[0] == SU_CLSU


            def u_1(g, tile0):
                dve.wait_ge(u_ready, g)
                v.tensor_tensor(q_prod[:, 0:3, :], u3[:, :, NS:NS + F], pe_var[:, tile0:tile0 + 3, 0:F], ALU.add)
                v.tensor_tensor(q_prod[:, 3:4, :], u1[:, :, NS:NS + F], pe_var[:, tile0 + 3:tile0 + 4, 0:F], ALU.add
                                ).then_inc(var_read, 1)

            def u_2(g, par):
                dve.wait_ge(var_read, g)
                v.tensor_tensor(q_prod[:, :, :], q_prod[:, :, :], x_in[:, par, :, :], ALU.mult).then_inc(v1[1], 1)

            def u_3(g):
                dve.wait_ge(v1[1], g)
                v.reduce_sum(q_sum[:, :], q_prod[:, :, :], axis=AX.X).then_inc(v1[0], 1)

            def u_4(g, tile0):
                dve.wait_ge(v1[0], g)
                v.scalar_tensor_tensor(ve1[:, :], q_sum[:, :], 1.0 / D, var_pe[:, tile0:tile0 + TPG, 1], ALU.mult, ALU.add
                                       ).then_inc(v1[2], 1)

            def u_5(g):
                dve.wait_ge(v1[2], g)
                v.tensor_scalar(ve1[:, :], ve1[:, :], 0.0, EPS, ALU.max, ALU.add).then_inc(v1[3], 1)

            def u_state(g, tile0):
                v.tensor_tensor(state_raw[:, 3:4, :], u1[:, :, 0:NS], pe_state[:, tile0 + 3:tile0 + 4, :], ALU.add)
                v.tensor_tensor(state_raw[:, 0:3, :], u3[:, :, 0:NS], pe_state[:, tile0:tile0 + 3, :], ALU.add
                                ).then_inc(state_read, 1)

            def newton(k, sems, n, t, sd, ve, nt):
                if k:
                    dve.wait_ge(sems[k - 1], n)
                if k == 0:
                    ins = v.reciprocal(t[:, 0, 0:nt], sd)
                elif k == 1:
                    ins = v.tensor_tensor(t[:, 1, 0:nt], t[:, 0, 0:nt], t[:, 0, 0:nt], ALU.mult)
                elif k == 2:
                    ins = v.scalar_tensor_tensor(t[:, 2, 0:nt], t[:, 1, 0:nt], -0.5, ve, ALU.mult, ALU.mult)
                else:
                    ins = v.scalar_tensor_tensor(t[:, 3, 0:nt], t[:, 2, 0:nt], 1.5, t[:, 0, 0:nt], ALU.add, ALU.mult)
                ins.then_inc(sems[k], 1)

            def newton1(k, g):
                if k == 0:
                    dve.wait_ge(sd1_ready, g)
                newton(k, v1[4:8], g, rs1, sd1[:, :], ve1[:, :], TPG)

            def newton2(k, g, nt):
                if k == 0:
                    dve.wait_ge(sd2_ready, g + 1)
                newton(k, v2[0:4], g + 1, rs2, sd2[:, 0:nt], ve2[:, 0:nt], nt)

            def u_scale(g, tile0):
                dve.wait_ge(v1[7], g)
                after(dve, scan_ready, g - 1)
                for c in range(TPG):
                    ins = v.scalar_tensor_tensor(state_in[:, c, :], state_raw[:, c, :], rs1[:, 3, c:c + 1],
                                                 inv_decay[:, tile0 + c, :], ALU.mult, ALU.mult)
                ins.then_inc(state_scaled, 1)

            def early_b(g, par, tile0):
                start = carry_cls[:, 0:1] if par else carry[:, 1, TPG - 1:TPG]
                after(dve, h_ready[TPG - 1], g - 2)
                dve.wait_ge(scan_ready, g)
                v.tensor_tensor_scan(carry[:, par, :], ones4[:, :], ps_scan[:, P - 1:GT:P], start, ALU.mult, ALU.add
                                     ).then_inc(carry_ready, 1)
                for c in range(TPG):
                    if c == 1:
                        dve.wait_ge(carry_ready, g)
                    ins = v.scalar_tensor_tensor(stateT[:, par, c * P:(c + 1) * P], ps_scan[:, c * P:(c + 1) * P],
                                                 start if c == 0 else carry[:, par, c - 1:c],
                                                 decayT[:, (tile0 + c) * P:(tile0 + c + 1) * P], ALU.add, ALU.mult)
                ins.then_inc(stateT_ready, 1)

            def h_add(g, par, tile0, c):
                if c == 0:
                    after(dve, o_scaled, g - 1)
                dve.wait_ge(h_ready[c], g)
                v.tensor_tensor(h1[:, par, c, :], ps_h[c % 2][:, :], pe_sb[:, tile0 + c, :], ALU.add
                                ).then_inc(h_added[c], 1)

            def h_bn(g, par, c):
                dve.wait_ge(h_added[c], g)
                ins = v.bn_stats(st2[:, c, :], h1[:, par, c, :])
                if c == TPG - 1:
                    ins.then_inc(h_stat, 1)

            def h_aggregate(g, nt):
                v.memset(feat[:, 0:nt, NFEAT - 1:NFEAT].bitcast(F32), 1.0)
                for c in range(nt):
                    ins = v.bn_aggr(mv2[:, c, :], st2[:, c, :])
                ins.then_inc(v2[4], 1)

            def h_eps(g, nt):
                dve.wait_ge(v2[4], g + 1)
                v.tensor_scalar(ve2[:, 0:nt], mv2[:, 0:nt, 1], EPS, None, ALU.add).then_inc(ve2_ready, 1)

            def h_norm(g, par, nt):
                T = slice(0, nt)
                dve.wait_ge(v2[3], g + 1)
                v.tensor_scalar(out_scale[:, par, T], rs2[:, 3, T], 1.0, None, ALU.add)
                v.scalar_tensor_tensor(out_bias[:, par, T], mv2[:, T, 0], -1.0, rs2[:, 3, T], ALU.mult, ALU.mult
                                       ).then_inc(scale_ready, 1)

            def h_y(g, par, nt):
                for c in range(nt):
                    ins = v.tensor_scalar(y[:, c, :], h1[:, par, c, 0:YC], mv2[:, c, 0:1], rs2[:, 3, c:c + 1],
                                          ALU.subtract, ALU.mult)
                ins.then_inc(y_done, 1)

            def features(g, par, nt):
                n, T = g + 1, slice(0, nt)
                dve.wait_ge(y_done, n)
                fields = y[:, T, ALU_LO:ALU_LO + FIELDS * NIB]
                weights = nib_w[:, :, :].rearrange("p f k -> p (f k)").unsqueeze(1).to_broadcast([P, nt, FIELDS * NIB])
                v.scalar_tensor_tensor(first_hit[:, T, :, :].rearrange("p c f k -> p c (f k)"), fields, HALF, weights,
                                       ALU.is_gt, ALU.mult).then_inc(hits_done, 1)
                v.tensor_scalar(marks[:, T, :], y[:, T, 0:3], HALF, None, ALU.is_gt).then_inc(marks_done, 1)
                v.tensor_copy(feat[:, T, 4:8:2], y[:, T, X_OP:X_OP + 2]).then_inc(op_hi_done, 1)
                dve.wait_ge(hits_done, n)
                v.reduce_max(hit_max[:, T, :], first_hit[:, T, :, :], axis=AX.X).then_inc(max_done, 1)
                dve.wait_ge(marks_done, n)
                v.tensor_tensor(both[:, T, :], marks[:, T, 1:3], marks[:, T, 0:1].to_broadcast([P, nt, 2]), ALU.mult
                                ).then_inc(both_done, 1)
                dve.wait_ge(op_hi_done, n)
                v.tensor_tensor(feat[:, T, 5:8:2], y[:, T, X_OP:X_OP + 2], feat[:, T, 4:8:2].bitcast(F32), ALU.subtract)
                dve.wait_ge(max_done, n)
                v.tensor_scalar(hit_pos[:, T, :], hit_max[:, T, :], -1.0, float(NIB), ALU.mult, ALU.add
                                ).then_inc(pos_done, 1)
                dve.wait_ge(both_done, n)
                v.tensor_copy(masks[:, par, T, 0], both[:, T, 0])
                v.tensor_tensor(masks[:, par, T, 1], both[:, T, 1], both[:, T, 0], ALU.is_gt).then_inc(masks_done, 1)
                dve.wait_ge(pos_done, n)
                v.scalar_tensor_tensor(feat[:, T, 0:4], hit_max[:, T, :], 0.0, hit_pos[:, T, :], ALU.is_gt, ALU.mult
                                       ).then_inc(feat_done, 1)
                dve.wait_ge(masks_done, n)
                v.tensor_tensor(active[:, par, T], masks[:, par, T, 0], masks[:, par, T, 1], ALU.add)
                dve.wait_ge(feat_done, n)
                after(dve, featT_ready, g)
                for m in range(2):
                    ins = v.tensor_tensor(
                        feat_rows[:, T, m * KF // 2:(m + 1) * KF // 2].rearrange("p c (d f) -> p c d f", d=2),
                        feat[:, T, :].bitcast(F32).unsqueeze(2).to_broadcast([P, nt, 2, NFEAT]),
                        masks[:, par, T, m:m + 1].unsqueeze(3).to_broadcast([P, nt, 2, NFEAT]), ALU.mult)
                ins.then_inc(rows_ready, 1)

            def k_step(k, s, par, nt):
                n, T = s + 1, slice(0, nt)
                if k == 0:
                    dve.wait_ge(y3_ready, n)
                    ins = v.tensor_tensor(y3m[:, T, :].rearrange("p c (o m) -> p c o m", m=2),
                                          ps_y[:, T, :].rearrange("p c (o m) -> p c o m", m=2),
                                          masks[:, par, T, :].unsqueeze(2).to_broadcast([P, nt, 3, 2]), ALU.mult)
                    ins.then_inc(p3[0], 1)
                    return
                dve.wait_ge(p3[k - 1], n)
                if k == 1:
                    ins = v.tensor_tensor(res[:, T, :], y3m[:, T, 0:6:2], y3m[:, T, 1:6:2], ALU.add)
                elif k == 2:
                    ins = v.tensor_scalar(res_c[:, T, :], res[:, T, 0:2], 0.0, float(NIB - 1), ALU.max, ALU.min)
                elif k == 3:
                    v.tensor_scalar(carry_out[:, T], res[:, T, 2], HALF, None, ALU.is_gt)
                    ins = v.tensor_scalar(res_up[:, T, :], res_c[:, T, :], MAGIC, None, ALU.add)
                elif k == 4:
                    ins = v.tensor_scalar(res_int[:, T, :], res_up[:, T, :], -MAGIC, None, ALU.add)
                elif k == 5:
                    ins = v.tensor_tensor(is_hot[:, T, :, :],
                                          hot[:, :].unsqueeze(1).unsqueeze(1).to_broadcast([P, nt, 2, NIB]),
                                          res_int[:, T, :].unsqueeze(3).to_broadcast([P, nt, 2, NIB]), ALU.is_equal)
                elif k == 6:
                    ins = v.scalar_tensor_tensor(is_hot2[:, T, :, :].rearrange("p c o k -> p c (o k)"),
                                                 is_hot[:, T, :, :].rearrange("p c o k -> p c (o k)"), 2.0,
                                                 active[:, par, T].unsqueeze(2).to_broadcast([P, nt, 2 * NIB]),
                                                 ALU.mult, ALU.mult)
                else:
                    dve.wait_ge(o_scaled, n)
                    lo = o_sb[:, par, T, OUT_LO:CARRY]
                    v.tensor_tensor(lo, lo, is_hot2[:, T, :, :].rearrange("p c o k -> p c (o k)"), ALU.add)
                    hi = o_sb[:, par, T, CARRY]
                    v.tensor_tensor(hi, hi, carry_out[:, T], ALU.add).then_inc(o_done, 1)
                    return
                ins.then_inc(p3[k], 1)

            def step(s, par, early=True, mid=True):
                cls = isinstance(s, int) and s == 0
                nt_before = 1 if isinstance(s, int) and s == 1 else TPG
                mt, et, mp = TPG * par, TPG * (1 - par), 1 - par
                k = lambda n: None if cls else k_step(n, s - 1, 1 - par, nt_before)
                if not mid:
                    for n in range(8):
                        k(n)
                    return
                h_add(s + 1, mp, mt, 0)
                h_add(s + 1, mp, mt, 1)
                h_bn(s + 1, mp, 0)
                k(0)
                h_bn(s + 1, mp, 1)
                k(1)
                h_add(s + 1, mp, mt, 2)
                k(2)
                h_bn(s + 1, mp, 2)
                k(3)
                h_add(s + 1, mp, mt, 3)
                k(4)
                if early:
                    u_1(s + 2, et)
                k(5)
                h_bn(s + 1, mp, 3)
                k(6)
                if early:
                    u_2(s + 2, par)
                k(7)
                dve.wait_ge(h_stat, s + 1)
                h_aggregate(s + 1, TPG)
                if early:
                    u_3(s + 2)
                h_eps(s + 1, TPG)
                if early:
                    u_4(s + 2, et)
                    u_state(s + 2, et)
                    u_5(s + 2)
                newton2(0, s + 1, TPG)
                for n in range(1, 4):
                    if early:
                        newton1(n - 1, s + 2)
                    newton2(n, s + 1, TPG)
                if early:
                    newton1(3, s + 2)
                if early:
                    u_scale(s + 2, et)
                h_norm(s + 1, mp, TPG)
                h_y(s + 1, mp, TPG)
                features(s + 1, mp, TPG)
                if early:
                    early_b(s + 2, par, et)

            u_1(1, 0)
            u_2(1, 1)
            u_3(1)
            u_4(1, 0)
            u_5(1)
            u_state(1, 0)
            for n in range(4):
                newton1(n, 1)
            dve.wait_ge(decay_ready, 1)
            u_scale(1, 0)
            dve.wait_ge(su_t, TS_CLSH)
            su(v.tensor_tensor(h1[:, 0, 0, :], bank[4][:, :], cls_sb[:, :], ALU.add))
            assert done[0] == SU_ALL
            v.bn_stats(st2[:, 0, :], h1[:, 0, 0, :]).then_inc(h_aggr, 1)
            dve.wait_ge(h_aggr, 1)
            h_aggregate(0, 1)
            h_eps(0, 1)
            for n in range(4):
                newton2(n, 0, 1)
            h_norm(0, 0, 1)
            h_y(0, 0, 1)
            features(0, 0, 1)
            early_b(1, 1, 0)
            step(0, 0)
            step(1, 1)
            step(2, 0)
            with dve.Fori(1, BATCH - 1) as b:
                step(2 * b + 1, 1)
                step(2 * b + 2, 0)
            step(GROUPS - 1, 1, early=False)
            step(GROUPS, 0, early=False, mid=False)
            for n in range(8):
                k_step(n, GROUPS, 0, TPG)

        @block.tensor
        def _(pe_):
            t = nc.tensor
            tile = lambda c: slice(c * P, (c + 1) * P)
            count = [0]

            def su(ins):
                count[0] += 1
                ins.then_inc(su_t, 1)

            pe_.wait_ge(const_step, IDENT)
            pe_.wait_ge(su_v, SU_CENTRED)
            for c in range(DC):
                t.transpose(bank[0][:, tile(c)], B_sb[:, tile(c)], ident[:, :])
            for c in range(DC):
                ins = t.transpose(bank[1][:, tile(c)], W4c[:, tile(c)], ident[:, :])
            su(ins)
            assert count[0] == TS_W
            pe_.wait_ge(ld_c, 16)
            for c in range(DC):
                ins = t.transpose(bank[3][:, tile(c)], C_sb[:, c, :], ident[:, :])
            su(ins)
            assert count[0] == TS_C
            pe_.wait_ge(su_v, SU_BW)
            for c in range(DC):
                ins = t.matmul(bank[2][:, 0:RG], W4T[:, c, :], BW[:, c, :], start=(c == 0), stop=(c == DC - 1))
            su(ins)
            assert count[0] == TS_R
            for k in range(TILES + 1):
                if k < TILES:
                    pe_.wait_ge(ld_pe[k // 2], 16)
                    if k >= 2:
                        pe_.wait_ge(su_a, pe_copied(k - 2))
                    for c in range(DC):
                        ins = t.transpose(bank[4 + k % 2][:, tile(c)], pe_sb[:, k, tile(c)], ident[:, :])
                    ins.then_inc(su_tp, 1)
                if k >= 1:
                    pe_.wait_ge(su_a, pe_copied(k - 1))
                    if k >= 3:
                        pe_.wait_ge(su_v, SU_PARTS + k - 2)
                    for c in range(DC):
                        ins = t.matmul(bank[6 + (k - 1) % 2][:, 0:RG], peT[:, (k - 1) % 2, tile(c)], BW[:, c, :],
                                       start=(c == 0), stop=(c == DC - 1))
                    su(ins)
            pe_.wait_ge(su_v, SU_CLSN)
            for c in range(DC):
                ins = t.transpose(bank[0][:, tile(c)], cls_n[:, tile(c)], ident[:, :])
            su(ins)
            assert count[0] == TS_CLST
            pe_.wait_ge(ld_f1, 16 * 8)
            pe_.wait_ge(spread_done, 6)
            pe_.wait_ge(su_v, SU_PE)
            for m in range(2):
                t.transpose(bank[5][:, tile(m)], top1[:, m, 0:P], ident[:, :])
                t.transpose(bank[5][:, 256 + REM * m:256 + REM * (m + 1)], bot1[:, m, 0:P], ident[0:REM, 0:REM])
                t.transpose(bank[4][:, tile(m)], spread1[:, m, :], ident[:, :])
            t.transpose(bank[5][:, 320:320 + P], diag1[:, :], ident[:, :])
            for k in range(8):
                ins = t.transpose(bank[6 + k // 4][0:KF, tile(k % 4)],
                                  zr[:, k, :, :, :].rearrange("p m d f -> p (m d f)").bitcast(F32), ident[:, :])
            su(ins)
            assert count[0] == TS_FFN
            pe_.wait_ge(su_v, SU_CLST)
            for c in range(DC):
                ins = t.matmul(bank[3][:, 0:P], BW[:, c, 0:NS], clsT[:, tile(c)], start=(c == 0), stop=(c == DC - 1))
            su(ins)
            assert count[0] == TS_CLSU
            pe_.wait_ge(const_step, CONSTS)

            def early_x(g, par):
                pe_.wait_ge(x_split, g)
                after(pe_, featT_copied, g - 1)
                for c in range(TPG):
                    ins = t.transpose(ps_T[:, tile(c)], x_parts[:, par, c, :, :].rearrange("p n k -> p (n k)").bitcast(F32),
                                      ident[:, :])
                ins.then_inc(xT_ready, 1)

            def early_u(g, par):
                pe_.wait_ge(xT_copied, g)
                after(pe_, state_read, g - 1)
                after(pe_, p3[0], g - 2)
                for c in range(TPG):
                    ins = t.matmul(u3[:, c, :] if c < 3 else ps_small[:, 0:RG], xT[:, par, tile(c)], r_x[:, :],
                                   start=True, stop=True)
                ins.then_inc(u_ready, 1)

            def early_s(g):
                pe_.wait_ge(state_scaled, g)
                after(pe_, stateT_ready, g - 1)
                for c in range(TPG):
                    ins = t.matmul(ps_scan[:, tile(c)], state_in[:, c, :], tri[:, :], start=True, stop=True)
                ins.then_inc(scan_ready, 1)

            def mid_h(g, par, c):
                if c == 0:
                    pe_.wait_ge(stateT_ready, g)
                if c >= 2:
                    pe_.wait_ge(h_added[c - 2], g)
                else:
                    after(pe_, h_added[c + 2], g - 1)
                t.matmul(ps_h[c % 2][:, :], xT[:, par, tile(c)], w_x[:, :], start=True, stop=False)
                t.matmul(ps_h[c % 2][:, :], stateT[:, par, tile(c)], CT[:, :], start=False, stop=True
                         ).then_inc(h_ready[c], 1)

            def back_f(s, nt):
                pe_.wait_ge(rows_ready, s + 1)
                after(pe_, xT_copied, min(s + 1, GROUPS) if isinstance(s, int) else s + 1)
                for c in range(nt):
                    ins = t.transpose(ps_T[:, tile(c)], feat_rows[:, c, :].bitcast(F32),
                                      ident[:, :])
                ins.then_inc(featT_ready, 1)

            def bank_free(s, k):
                if k >= 2:
                    pe_.wait_ge(f_relu[k - 2], s + 1)
                else:
                    after(pe_, f_relu[k + 6], s)

            def back_1(s, k, n):
                if k == 0:
                    pe_.wait_ge(featT_copied, s + 1)
                bank_free(s, k)
                t.matmul(ps_f[k % 2][:, 0:n], w_feat[:, k, :], featT[:, 0:n], start=True, stop=True).then_inc(f_ready[k], 1)

            def back_2(s, q, n):
                k = 5 + q
                bank_free(s, k)
                o = ps_f[k % 2][:, 0:n]
                t.matmul(o, w_feat[:, k, :], featT[:, 0:n], start=True, stop=False)
                for m in range(2):
                    t.matmul(o, w2_main[:, m, :], hid1[:, 2 * q + m, 0:n], start=False, stop=False)
                pe_.wait_ge(f_relu[4], s + 1)
                t.matmul(o, w2_rem_main[:, q, :], hid1[:, 4, 0:n], start=False, stop=True).then_inc(f_ready[k], 1)

            def back_2r(s, n):
                bank_free(s, 7)
                o = ps_f[1][:, 0:n]
                t.matmul(o, w2_rem[:, :], hid1[:, 4, 0:n], start=True, stop=False)
                for k in range(4):
                    ins = t.matmul(ps_f[1][REM * k:REM * (k + 1), 0:n], w2_main_rem[:, k % 2, :], hid1[:, k, 0:n],
                                   start=False, stop=True)
                ins.then_inc(f_ready[7], 1)

            def back_3(s, n, early_g):
                pe_.wait_ge(f_relu[7], s + 1)
                after(pe_, state_read, early_g)
                after(pe_, p3[0], s)
                for k in range(3):
                    ins = t.matmul(ps_small[REM * k:REM * (k + 1), 0:n], w3[:, k, :], hid2[:, k, 0:n], start=True, stop=True)
                ins.then_inc(y3_parts, 1)

            def back_4(s, nt):
                pe_.wait_ge(y3_copied, s + 1)
                for c in range(nt):
                    ins = t.matmul(ps_y[:, c, :], y3T[:, tile(c)], pick3[:, :], start=True, stop=True)
                ins.then_inc(y3_ready, 1)

            def step(s, par, early=True, mid=True):
                cls = isinstance(s, int) and s == 0
                nt, n = (1, P) if cls else (TPG, GT)
                back_f(s, nt)
                if mid:
                    mid_h(s + 1, 1 - par, 0)
                    mid_h(s + 1, 1 - par, 1)
                if not cls:
                    back_4(s - 1, 1 if isinstance(s, int) and s == 1 else TPG)
                back_1(s, 0, n)
                back_1(s, 1, n)
                if early:
                    early_x(s + 2, par)
                if mid:
                    mid_h(s + 1, 1 - par, 2)
                back_1(s, 2, n)
                back_1(s, 3, n)
                if mid:
                    mid_h(s + 1, 1 - par, 3)
                if early:
                    early_u(s + 2, par)
                back_1(s, 4, n)
                back_2(s, 0, n)
                back_2(s, 1, n)
                back_2r(s, n)
                if early:
                    early_s(s + 2)
                back_3(s, n, s + 2 if early else GROUPS)

            early_x(1, 1)
            early_u(1, 1)
            pe_.wait_ge(su_v, SU_CLSU)
            pe_.wait_ge(su_a, SA_FFN)
            su(t.matmul(bank[4][:, :], stateT_cls[:, :], CT[:, :], start=True, stop=True))
            assert count[0] == TS_CLSH
            early_s(1)
            pe_.wait_ge(su_v, SU_ALL)
            pe_.wait_ge(ld_f3, 16 * 18)
            step(0, 0)
            step(1, 1)
            step(2, 0)
            with pe_.Fori(1, BATCH - 1) as b:
                step(2 * b + 1, 1)
                step(2 * b + 2, 0)
            step(GROUPS - 1, 1, early=False)
            step(GROUPS, 0, early=False, mid=False)
            back_4(GROUPS, TPG)


_INS = ["x", "cls_tok", "L0_tok_W", "L0_attn_log_lambda", "L0_attn_B", "L0_attn_C", "L0_attn_log_dt",
        "L0_ffn_Wa", "L0_ffn_ba", "L0_ffn_Ws", "L0_ffn_bs"]


def kernel(**inputs):
    import concourse.bacc as bacc
    from concourse.bass_utils import run_bass_kernel_spmd

    nc = bacc.Bacc("TRN2", target_bir_lowering=False, num_devices=1)
    arrays, args = {}, []

    def give(name, a):
        arrays[name] = a
        args.append(nc.dram_tensor(name, a.shape, mybir.dt.from_np(a.dtype), kind="ExternalInput").ap())

    for name in _INS:
        a = np.ascontiguousarray(inputs[name])
        give(f"in_{name}", a.reshape(1) if a.ndim == 0 else a)
    batch, height, width, _ = arrays["in_x"].shape
    d_model = arrays["in_L0_tok_W"].shape[1]
    give("pe", position_table(height * width, d_model))
    out = nc.dram_tensor("out", (batch, height * width + 1, d_model), F32, kind="ExternalOutput").ap()
    vit_layer(nc, *args, out)
    r = run_bass_kernel_spmd(nc, [arrays], core_ids=[0])
    return r.results[0]["out"]
```

```python
import math
from contextlib import ExitStack

import numpy as np
import concourse.bass as bass
from concourse import mybir

F32 = mybir.dt.float32
F32R = mybir.dt.float32r
ALU = mybir.AluOpType
ACT = mybir.ActivationFunctionType
AX = mybir.AxisListType


def position_table(seq_len, d_model):
    position = np.arange(seq_len, dtype=np.float32)[:, None]
    div_term = np.exp(np.arange(0, d_model, 2, dtype=np.float32) * (-math.log(10000.0) / d_model))
    pe = np.zeros((seq_len, d_model), dtype=np.float32)
    pe[:, 0::2] = np.sin(position * div_term)
    pe[:, 1::2] = np.cos(position * div_term)
    return pe


def after(eng, sem, count):
    if isinstance(count, int) and count <= 0:
        return
    eng.wait_ge(sem, count)


SU_CENTRED, SU_BW, SU_CLSVE, SU_CLSN, SU_PARTS, SU_PE, SU_VAR, SU_CLST, SU_CLSU, SU_H, SU_ALL = (
    6, 7, 10, 15, 19, 27, 28, 29, 30, 31, 32)
TS_W, TS_C, TS_R, TS_PE, TS_CLST, TS_CLSU, TS_FFN, TS_CLSH = 1, 2, 3, 3, 12, 13, 14, 15
SA_ROOT, SA_C, SA_EXP, SA_REM, SA_FFN = 3, 4, 14, 15, 17
IDENT, CONSTS = 4, 21


def vit_layer(nc, x, cls_tok, tok_w, log_lambda, B, C, log_dt, Wa, ba, Ws, bs, pe, out):
    P = 128
    BATCH, GRID_H, GRID_W, F = x.shape
    D = tok_w.shape[1]
    NS = B.shape[0]
    TOK = GRID_H * GRID_W
    TPG = 4
    GT = TPG * P
    TILES = TOK // P
    GROUPS = BATCH * TOK // GT
    DC = D // P
    BLK = 32
    NB = P // BLK
    RG = NS + BLK
    GE = Wa.shape[1]
    REM = GE - P
    EPS = 1e-5
    HALF = 0.5
    NIB_A, OPC_ADD, ALU_LO, OP_START = 0, 25, 16, 10
    IN_OP = OP_START + OPC_ADD
    X_OP = 80 + OPC_ADD
    FIELDS, NIB = 4, 16
    YC = X_OP + 2
    RESULT = 100
    OUT_LO, CARRY, RES_END = 128, 160, 192
    LO_ROW = 8
    NFEAT = 9
    KF = 2 * 2 * NFEAT
    MAGIC = 1.5 * 2.0 ** 23
    assert D == 512 and NS == P and F <= BLK - 1 and TILES == 2 * TPG and REM == 32

    xf = x.rearrange("b h w f -> (b h w) f")
    pipes = ((Wa, ba), (Ws, bs))

    ctx = ExitStack()
    with ctx:
        def sb(name, shape, dt=F32):
            return ctx.enter_context(nc.sbuf_tensor(name, shape, dt))

        def sem(name):
            return ctx.enter_context(nc.semaphore(name))

        ident = sb("ident", [P, P])
        tri = sb("tri", [P, P])
        pe_sb = sb("pe_sb", [P, TILES, D])
        pe_state = sb("pe_state", [P, TILES, NS])
        pe_var = sb("pe_var", [P, TILES, BLK])
        var_pe = sb("var_pe", [P, TILES, 2])
        decayT = sb("decayT", [P, TOK])
        inv_decay = sb("inv_decay", [P, TILES, NS])
        w_x = sb("w_x", [P, D], F32R)
        r_x = sb("r_x", [P, RG], F32R)
        CT = sb("CT", [P, D])
        w_feat = sb("w_feat", [KF, 8, P], F32R)
        w2_main = sb("w2_main", [P, 2, P])
        w2_main_rem = sb("w2_main_rem", [P, 2, REM])
        w2_rem_main = sb("w2_rem_main", [P, 2, P])
        w2_rem = sb("w2_rem", [P, P])
        w3 = sb("w3", [P, 3, REM])
        b3 = sb("b3", [3 * REM, 1])
        lo_row = sb("lo_row", [3 * REM, 1])
        pick3 = sb("pick3", [3 * REM, 6], F32R)
        nib_w = sb("nib_w", [P, FIELDS, NIB])
        hot = sb("hot", [P, NIB])
        ones4 = sb("ones4", [P, TPG])
        pick_hi = sb("pick_hi", [3 * REM, 6])
        pick_lo = sb("pick_lo", [3 * REM, 6])
        carry_cls = sb("carry_cls", [P, 1])
        B_sb = sb("B_sb", [P, D])
        C_sb = sb("C_sb", [P, DC, P])
        W4 = sb("W4", [P, D])
        W4c = sb("W4c", [P, D])
        w_hi = sb("w_hi", [P, D], F32R)
        r_all = sb("r_all", [P, RG])
        r_hi = sb("r_hi", [P, RG], F32R)
        BW = sb("BW", [P, DC, RG])
        W4T = sb("W4T", [P, DC, P])
        peT = sb("peT", [P, 2, D])
        mean_b = sb("mean_b", [P, 1])
        mean_w = sb("mean_w", [P, 1])
        stat_pe = sb("stat_pe", [P, TILES, 6])
        ll_col = sb("ll_col", [P, 2])
        ll_row = sb("ll_row", [P, NS])
        ld_col = sb("ld_col", [P, 1])
        ld_row = sb("ld_row", [P, NS])
        t_row = sb("t_row", [P, TOK])
        t_col = sb("t_col", [P, TILES])
        top1 = sb("top1", [P, 2, GE])
        bot1 = sb("bot1", [REM, 2, GE])
        diag1 = sb("diag1", [P, P])
        spread1 = sb("spread1", [P, 2, P])
        top0 = sb("top0", [P, 2, GE])
        rem0 = sb("rem0", [P, GE])
        bias_main = sb("bias_main", [P, 2, 2])
        bias_rem = sb("bias_rem", [P, 2])
        zf = sb("zf", [P, 8, 2, NFEAT])
        zr = sb("zr", [P, 8, 2, 2, NFEAT], F32R)
        cls_sb = sb("cls_sb", [P, D])
        cls_st = sb("cls_st", [P, 6])
        cls_mv = sb("cls_mv", [P, 2])
        cls_ve = sb("cls_ve", [P, 1])
        cls_sd = sb("cls_sd", [P, 1])
        cls_r = sb("cls_r", [P, 4])
        cls_n = sb("cls_n", [P, D])
        clsT = sb("clsT", [P, D])
        stateT_cls = sb("stateT_cls", [P, P])
        x_in = sb("x_in", [P, 2, TPG, F])
        x_parts = sb("x_parts", [P, 2, TPG, NB, BLK], F32R)
        xT = sb("xT", [P, 2, GT], F32R)
        q_prod = sb("q_prod", [P, TPG, F])
        q_sum = sb("q_sum", [P, TPG])
        ve1 = sb("ve1", [P, TPG])
        sd1 = sb("sd1", [P, TPG])
        rs1 = sb("rs1", [P, 4, TPG])
        state_raw = sb("state_raw", [P, TPG, NS])
        state_in = sb("state_in", [P, TPG, NS])
        carry = sb("carry", [P, 2, TPG])
        stateT = sb("stateT", [P, 2, GT])
        h1 = sb("h1", [P, 2, TPG, D])
        st2 = sb("st2", [P, TPG, 6])
        mv2 = sb("mv2", [P, TPG, 2])
        ve2 = sb("ve2", [P, TPG])
        sd2 = sb("sd2", [P, TPG])
        rs2 = sb("rs2", [P, 4, TPG])
        out_scale = sb("out_scale", [P, 2, TPG])
        out_bias = sb("out_bias", [P, 2, TPG])
        y = sb("y", [P, TPG, YC])
        first_hit = sb("first_hit", [P, TPG, FIELDS, NIB])
        hit_max = sb("hit_max", [P, TPG, FIELDS])
        hit_pos = sb("hit_pos", [P, TPG, FIELDS])
        marks = sb("marks", [P, TPG, 3])
        both = sb("both", [P, TPG, 2])
        masks = sb("masks", [P, 2, TPG, 2])
        active = sb("active", [P, 2, TPG])
        feat = sb("feat", [P, TPG, NFEAT], F32R)
        feat_rows = sb("feat_rows", [P, TPG, P], F32R)
        featT = sb("featT", [KF, GT], F32R)
        hid1 = sb("hid1", [P, 5, GT])
        hid2 = sb("hid2", [P, 3, GT])
        y3_hi = sb("y3_hi", [3 * REM, GT], F32R)
        y3T = sb("y3T", [3 * REM, GT], F32R)
        y3m = sb("y3m", [P, TPG, 6])
        res = sb("res", [P, TPG, 3])
        res_c = sb("res_c", [P, TPG, 2])
        res_up = sb("res_up", [P, TPG, 2])
        res_int = sb("res_int", [P, TPG, 2])
        is_hot = sb("is_hot", [P, TPG, 2, NIB])
        active2 = sb("active2", [P, TPG])
        is_hot2 = sb("is_hot2", [P, TPG, 2, NIB])
        carry_out = sb("carry_out", [P, TPG])
        o_sb = sb("o_sb", [P, 2, TPG, D])

        bank = [ctx.enter_context(nc.psum_tensor(f"bank{n}", [P, 512], F32)) for n in range(8)]
        ps_T, ps_small, ps_state, ps_scan = bank[0], bank[1], bank[2], bank[3]
        ps_h, ps_f = bank[4:6], bank[6:8]
        u3 = ps_state[:, 0:3 * RG].rearrange("p (c k) -> p c k", c=3)
        u1 = ps_small[:, 0:RG].unsqueeze(1)
        ps_y = ps_small[:, 0:TPG * 6].rearrange("p (c k) -> p c k", c=TPG)

        ld_b, ld_w, ld_c, ld_lam, ld_cls = (sem(n) for n in ("ld_b", "ld_w", "ld_c", "ld_lam", "ld_cls"))
        ld_pe = [sem(f"ld_pe{n}") for n in range(TILES // 2)]
        ld_f1, ld_f0, ld_f3 = sem("ld_f1"), sem("ld_f0"), sem("ld_f3")
        zeroed = sem("zeroed")
        const_step = sem("const_step")
        su_v = sem("su_v")
        su_a = sem("su_a")
        su_tp = sem("su_tp")
        su_t = sem("su_t")
        clip_step = sem("clip_step")
        decay_ready = sem("decay_ready")
        spread_done = sem("spread_done")
        l3_step = sem("l3_step")
        x_loaded = [sem("x_loaded0"), sem("x_loaded1")]
        x_hi = sem("x_hi")
        x_split, xT_ready, xT_copied = sem("x_split"), sem("xT_ready"), sem("xT_copied")
        u_ready, var_read, state_read = sem("u_ready"), sem("var_read"), sem("state_read")
        v1 = [sem(f"v1_{n}") for n in range(8)]
        sd1_ready = sem("sd1_ready")
        state_scaled, scan_ready, carry_ready, stateT_ready = sem("state_scaled"), sem("scan_ready"), sem("carry_ready"), sem("stateT_ready")
        h_ready = [sem(f"h_ready{c}") for c in range(TPG)]
        h_added = [sem(f"h_added{c}") for c in range(TPG)]
        h_stat, h_aggr = sem("h_stat"), sem("h_aggr")
        v2 = [sem(f"v2_{n}") for n in range(5)]
        ve2_ready, sd2_ready, scale_ready = sem("ve2_ready"), sem("sd2_ready"), sem("scale_ready")
        y_done, hits_done, max_done, pos_done, op_hi_done, marks_done, both_done, masks_done, feat_done = (
            sem(n) for n in ("y_done", "hits_done", "max_done", "pos_done", "op_hi_done", "marks_done",
                             "both_done", "masks_done", "feat_done"))
        rows_ready, featT_ready, featT_copied = sem("rows_ready"), sem("featT_ready"), sem("featT_copied")
        f_ready = [sem(f"f_ready{k}") for k in range(8)]
        f_relu = [sem(f"f_relu{k}") for k in range(8)]
        y3_parts, y3_rounded, y3_split, y3_ready = (sem(n) for n in ("y3_parts", "y3_rounded", "y3_split", "y3_ready"))
        p3 = [sem(f"p3_{n}") for n in range(8)]
        o_scaled, o_done = sem("o_scaled"), sem("o_done")
        o_stored = [sem("o_stored0"), sem("o_stored1")]

        block = ctx.enter_context(nc.Block())

        def load_x(eng, g, row, par):
            after(eng, x_split, g - 2)
            after(eng, v1[1], g - 2)
            eng.dma_start(x_in[:, par, :, :], xf[bass.ds(row, GT), :].rearrange("(c p) f -> p c f", p=P)
                          ).then_inc(x_loaded[par], 16)

        def store(eng, g, b, half, par):
            after(eng, o_done, g + 1)
            eng.dma_start(out[b, 1 + half * GT:1 + (half + 1) * GT, :].rearrange("(c p) d -> p c d", p=P),
                          o_sb[:, par, :, :]).then_inc(o_stored[par], 16)

        @block.sync
        def _(sp):
            sp.dma_start(B_sb[:, :], B).then_inc(ld_b, 16)
            sp.wait_ge(zeroed, 1)
            for n in range(NB):
                sp.dma_start(W4[n * BLK:n * BLK + F, :], tok_w).then_inc(ld_w, 16)
            for c in range(0, TILES, 2):
                sp.dma_start(pe_sb[:, c:c + 2, :], pe[c * P:(c + 2) * P, :].rearrange("(c p) d -> p c d", p=P)
                             ).then_inc(ld_pe[c // 2], 16)
            sp.dma_start(cls_sb[:, :], cls_tok[0, :, :].to_broadcast([P, D])).then_inc(ld_cls, 16)
            load_x(sp, 1, 0, 1)
            load_x(sp, 2, GT, 0)
            sp.wait_ge(zeroed, 4)
            for m, (w, bb) in enumerate(pipes):
                sp.dma_start(top1[:, m, :], w[1, 0:P, :]).then_inc(ld_f1, 16)
                sp.dma_start(bot1[:, m, :], w[1, P:GE, :]).then_inc(ld_f1, 16)
                sp.dma_start(top0[:, m, :], w[0, 0:P, :]).then_inc(ld_f0, 16)
                sp.dma_start(bias_main[:, :, m:m + 1], bb[0:2, 0:P].rearrange("l (p o) -> p l o", o=1),
                             allow_slow_non_contiguous=True).then_inc(ld_f0, 16)
            for q in range(2):
                for m, (w, bb) in enumerate(pipes):
                    r = slice(REM * (2 * q + m), REM * (2 * q + m + 1))
                    sp.dma_start(diag1[r, r], w[1, P:GE, P:GE]).then_inc(ld_f1, 16)
                    sp.dma_start(rem0[r, :], w[0, P:GE, :]).then_inc(ld_f0, 16)
                    sp.dma_start(bias_rem[r, :].unsqueeze(2), bb[0:2, P:GE].rearrange("l (p o) -> p l o", o=1),
                                 allow_slow_non_contiguous=True).then_inc(ld_f0, 16)
            for m, (w, bb) in enumerate(pipes):
                for o, row, q in ((0, RESULT, 0), (1, RESULT, 1), (2, RESULT + 1, 1)):
                    col = 2 * o + m
                    r = slice(REM * (2 * q + m), REM * (2 * q + m + 1))
                    sp.dma_start(w3[:, q, col:col + 1], w[2, row, 0:P].unsqueeze(1),
                                 allow_slow_non_contiguous=True).then_inc(ld_f3, 16)
                    sp.dma_start(w3[r, 2, col:col + 1], w[2, row, P:GE].unsqueeze(1),
                                 allow_slow_non_contiguous=True).then_inc(ld_f3, 16)
                    for first in (col, LO_ROW + col):
                        sp.dma_start(b3[first:first + 1, :], bb[2, row:row + 1].unsqueeze(0)).then_inc(ld_f3, 16)
            load_x(sp, 3, 2 * GT, 1)
            load_x(sp, 4, 3 * GT, 0)
            sp.wait_ge(o_done, 1)
            sp.dma_start(out[:, 0, :], o_sb[0:BATCH, 0, 0, :]).then_inc(o_stored[0], 16)
            load_x(sp, 5, 4 * GT, 1)
            store(sp, 1, 0, 0, 1)
            load_x(sp, 6, 5 * GT, 0)
            store(sp, 2, 0, 1, 0)
            with sp.Fori(1, BATCH - 2) as b:
                for half in range(2):
                    load_x(sp, 2 * b + 5 + half, (2 * b + 4 + half) * GT, 1 - half)
                    store(sp, 2 * b + 1 + half, b, half, 1 - half)
            store(sp, GROUPS - 3, BATCH - 2, 0, 1)
            store(sp, GROUPS - 2, BATCH - 2, 1, 0)
            store(sp, GROUPS - 1, BATCH - 1, 0, 1)
            sp.wait_ge(o_scaled, GROUPS + 1)
            last = out[BATCH - 1, 1 + GT:1 + 2 * GT, :].rearrange("(c p) d -> p c d", p=P)
            for cols in (slice(0, OUT_LO), slice(RES_END, D)):
                sp.dma_start(last[:, :, cols], o_sb[:, 0, :, cols]).then_inc(o_stored[0], 16)
            sp.wait_ge(o_done, GROUPS + 1)
            sp.dma_start(last[:, :, OUT_LO:RES_END], o_sb[:, 0, :, OUT_LO:RES_END]).then_inc(o_stored[0], 16)
            sp.wait_ge(o_stored[1], 16 * BATCH)
            sp.wait_ge(o_stored[0], 16 * (BATCH + 3))

        @block.gpsimd
        def _(pool):
            g = nc.gpsimd
            g.memset(W4[:, :], 0.0).then_inc(zeroed, 1)
            g.memset(ident[:, :], 0.0).then_inc(const_step, 1)
            g.memset(tri[:, :], 1.0).then_inc(const_step, 1)
            g.memset(diag1[:, :], 0.0).then_inc(zeroed, 1)
            g.memset(w3[:, :, :], 0.0).then_inc(zeroed, 1)
            g.memset(b3[:, :], 0.0).then_inc(zeroed, 1)
            pool.wait_ge(const_step, 2)
            g.affine_select(out=ident[:, :], in_=ident[:, :], compare_op=ALU.not_equal, fill=1.0, base=0,
                            pattern=[[-1, P]], channel_multiplier=1).then_inc(const_step, 1)
            g.affine_select(out=tri[:, :], in_=tri[:, :], compare_op=ALU.is_ge, fill=0.0, base=0,
                            pattern=[[1, P]], channel_multiplier=-1).then_inc(const_step, 1)
            imp = dict(allow_small_or_imprecise_dtypes=True)
            g.iota(t_row[:, :], pattern=[[1, TOK]], base=1, channel_multiplier=0, **imp).then_inc(const_step, 1)
            g.iota(t_col[:, :], pattern=[[P, TILES]], base=1, channel_multiplier=1, **imp).then_inc(const_step, 1)
            g.iota(nib_w[:, :, :], pattern=[[0, FIELDS], [-1, NIB]], base=NIB, channel_multiplier=0, **imp).then_inc(const_step, 1)
            g.iota(hot[:, :], pattern=[[1, NIB]], base=0, channel_multiplier=0, **imp).then_inc(const_step, 1)
            g.memset(x_parts[:, :, :, :, :].bitcast(F32), 0.0).then_inc(const_step, 1)
            g.memset(zf[:, :, :, :], 0.0).then_inc(const_step, 1)
            g.memset(spread1[:, :, :], 0.0).then_inc(const_step, 1)
            g.memset(ones4[:, :], 1.0).then_inc(const_step, 1)
            g.memset(feat_rows[:, :, :].bitcast(F32), 0.0).then_inc(const_step, 1)
            g.memset(pick_hi[:, :], 0.0).then_inc(const_step, 1)
            g.memset(pick_lo[:, :], 0.0).then_inc(const_step, 1)
            for k in range(3):
                pool.wait_ge(const_step, CONSTS - 6 + 2 * k)
                for pick, base in ((pick_hi, REM * k), (pick_lo, REM * k + LO_ROW)):
                    g.affine_select(out=pick[:, :], in_=pick[:, :], compare_op=ALU.not_equal, fill=1.0, base=-base,
                                    pattern=[[-1, 6]], channel_multiplier=1).then_inc(const_step, 1)
            pool.wait_ge(const_step, CONSTS)

            def split_x(n, par):
                after(pool, x_loaded[par], 16 * n["load"])
                after(pool, xT_ready, n["g"] - 2)
                parts, xin = x_parts[:, par, :, :, :], x_in[:, par, :, :]
                g.tensor_tensor(parts[:, :, 0, 0:F], xin, ones4[:, :].unsqueeze(2).to_broadcast([P, TPG, F]), ALU.mult).then_inc(x_hi, 1)
                g.tensor_copy(parts[:, :, 2, 0:F], xin).then_inc(x_hi, 1)
                after(pool, x_hi, 2 * n["g"])
                g.tensor_tensor(parts[:, :, 1, 0:F], xin, parts[:, :, 0, 0:F].bitcast(F32), ALU.subtract)
                g.tensor_tensor(parts[:, :, 3, 0:F], xin, parts[:, :, 0, 0:F].bitcast(F32), ALU.subtract
                                ).then_inc(x_split, 1)

            pool.wait_ge(su_a, 2)
            g.tensor_scalar(ld_col[:, :], ll_col[:, 0:1], ll_col[:, 1:2], -1.0, ALU.mult, ALU.mult).then_inc(clip_step, 1)
            g.tensor_scalar(ld_row[:, :], ll_row[:, :], ll_col[:, 1:2], -1.0, ALU.mult, ALU.mult).then_inc(clip_step, 1)
            pool.wait_ge(clip_step, 2)
            for c in range(TILES):
                g.tensor_scalar(inv_decay[:, c, :], ld_row[:, :], t_col[:, c:c + 1], -30.0, ALU.mult, ALU.max
                                ).then_inc(clip_step, 1)
            g.tensor_scalar(decayT[:, :], t_row[:, :], ld_col[:, 0:1], -30.0, ALU.mult, ALU.max).then_inc(clip_step, 1)
            pool.wait_ge(clip_step, 3 + TILES)
            g.tensor_scalar(inv_decay[:, :, :], inv_decay[:, :, :], 0.0, None, ALU.min).then_inc(clip_step, 1)
            g.tensor_scalar(decayT[:, :], decayT[:, :], 0.0, None, ALU.min).then_inc(clip_step, 1)
            split_x(dict(g=1, load=1), 1)
            split_x(dict(g=2, load=1), 0)
            pool.wait_ge(su_a, SA_EXP)
            g.tensor_scalar(inv_decay[:, :, :], inv_decay[:, :, :], 1e6, None, ALU.min).then_inc(decay_ready, 1)
            split_x(dict(g=3, load=2), 1)
            split_x(dict(g=4, load=2), 0)

            def write_result(s, par, nt):
                n, T = s + 1, slice(0, nt)
                pool.wait_ge(p3[5], n)
                g.tensor_tensor(active2[:, T], active[:, par, T], active[:, par, T], ALU.add).then_inc(p3[7], 1)
                pool.wait_ge(p3[7], n)
                g.tensor_tensor(is_hot2[:, T, :, :].rearrange("p c o k -> p c (o k)"),
                                is_hot[:, T, :, :].rearrange("p c o k -> p c (o k)"),
                                active2[:, T].unsqueeze(2).to_broadcast([P, nt, 2 * NIB]), ALU.mult).then_inc(p3[6], 1)
                pool.wait_ge(p3[6], n)
                pool.wait_ge(o_scaled, n)
                lo, hi = o_sb[:, par, T, OUT_LO:CARRY], o_sb[:, par, T, CARRY]
                g.tensor_tensor(lo, lo, is_hot2[:, T, :, :].rearrange("p c o k -> p c (o k)"), ALU.add)
                g.tensor_tensor(hi, hi, carry_out[:, T], ALU.add).then_inc(o_done, 1)

            write_result(0, 0, 1)
            split_x(dict(g=5, load=3), 1)
            write_result(1, 1, TPG)
            split_x(dict(g=6, load=3), 0)
            with pool.Fori(2, BATCH - 1) as b:
                for half in range(2):
                    write_result(2 * b - 2 + half, half, TPG)
                    split_x(dict(g=2 * b + 3 + half, load=b + 2), 1 - half)
            for n in range(GROUPS - 4, GROUPS + 1):
                write_result(n, n % 2, TPG)

        @block.scalar
        def _(act):
            a = nc.scalar
            act.dma_start(ll_col[:, 0:1], log_lambda.unsqueeze(1)).then_inc(ld_lam, 16)
            act.dma_start(ll_row[:, :], log_lambda.unsqueeze(0).to_broadcast([P, NS])).then_inc(ld_lam, 16)
            act.dma_start(ll_col[:, 1:2], log_dt.unsqueeze(0).to_broadcast([P, 1])).then_inc(ld_lam, 16)
            act.dma_start(C_sb[:, :, :], C.rearrange("(c p) n -> p c n", p=P)).then_inc(ld_c, 16)
            act.wait_ge(ld_lam, 48)
            a.activation(ll_col[:, :], ll_col[:, :], ACT.Exp).then_inc(su_a, 1)
            a.activation(ll_row[:, :], ll_row[:, :], ACT.Exp).then_inc(su_a, 1)
            act.wait_ge(su_v, SU_CLSVE)
            a.activation(cls_sd[:, :], cls_ve[:, :], ACT.Sqrt).then_inc(su_a, 1)
            act.wait_ge(su_t, TS_C)
            a.copy(CT[:, :], bank[3][:, :]).then_inc(su_a, 1)
            for c in range(TILES):
                act.wait_ge(su_tp, c + 1)
                if c >= 2:
                    act.wait_ge(su_t, TS_PE + c - 1)
                a.copy(peT[:, c % 2, :], bank[4 + c % 2][:, :]).then_inc(su_a, 1)
            act.wait_ge(clip_step, 5 + TILES)
            a.activation(decayT[:, :], decayT[:, :], ACT.Exp).then_inc(su_a, 1)
            a.activation(inv_decay[:, :, :], inv_decay[:, :, :], ACT.Exp, scale=-1.0).then_inc(su_a, 1)

            def copy_featT(s):
                n = P if isinstance(s, int) and s == 0 else GT
                act.wait_ge(featT_ready, s + 1)
                a.copy(featT[:, 0:n], ps_T[0:KF, 0:n]).then_inc(featT_copied, 1)

            def relu(s, k):
                n = P if isinstance(s, int) and s == 0 else GT
                act.wait_ge(f_ready[k], s + 1)
                dst = hid1[:, k, 0:n] if k < 5 else hid2[:, k - 5, 0:n]
                a.activation(dst, ps_f[k % 2][:, 0:n], ACT.Relu, bias=bias_rem[:, 1:2] if k == 7 else 0.0
                             ).then_inc(f_relu[k], 1)

            def copy_xT(g, par):
                act.wait_ge(xT_ready, g)
                after(act, h_ready[TPG - 1], g - 2)
                a.copy(xT[:, par, :], ps_T[:, :]).then_inc(xT_copied, 1)

            def sqrt1(g):
                act.wait_ge(v1[3], g)
                a.activation(sd1[:, :], ve1[:, :], ACT.Sqrt).then_inc(sd1_ready, 1)

            def sqrt2(g, nt):
                act.wait_ge(ve2_ready, g + 1)
                a.activation(sd2[:, 0:nt], ve2[:, 0:nt], ACT.Sqrt).then_inc(sd2_ready, 1)

            def scale_out(s, par, tiles, nstore, last):
                act.wait_ge(scale_ready, s + 1)
                after(act, o_stored[par], 16 * nstore)
                for c in tiles:
                    ins = a.activation(o_sb[:, par, c, :], h1[:, par, c, :], ACT.Identity,
                                       bias=out_bias[:, par, c:c + 1], scale=out_scale[:, par, c:c + 1])
                if last:
                    ins.then_inc(o_scaled, 1)

            def step(s, par, nstore, x_part=True, early=True, mid=True):
                cls = isinstance(s, int) and s == 0
                relu(s, 0)
                relu(s, 1)
                relu(s, 2)
                relu(s, 3)
                if early:
                    sqrt1(s + 2)
                relu(s, 4)
                scale_out(s, par, range(1 if cls else 2), nstore, cls)
                if mid:
                    sqrt2(s + 1, TPG)
                relu(s, 5)
                if not cls:
                    scale_out(s, par, range(2, TPG), nstore, True)
                relu(s, 6)
                if x_part:
                    copy_xT(s + 3, 1 - par)
                relu(s, 7)
                if mid:
                    copy_featT(s + 1)

            a.activation(sd1[:, 0:1], cls_ve[:, :], ACT.Sqrt)
            copy_xT(1, 1)
            act.wait_ge(su_t, TS_FFN)
            a.copy(w2_rem_main[:, :, :], bank[4][:, 0:2 * P].rearrange("p (m k) -> p m k", m=2)).then_inc(su_a, 1)
            a.copy(w_feat[:, 0:4, :], bank[6][0:KF, :].rearrange("p (m k) -> p m k", m=4)).then_inc(su_a, 1)
            a.copy(w_feat[:, 4:8, :], bank[7][0:KF, :].rearrange("p (m k) -> p m k", m=4)).then_inc(su_a, 1)
            sqrt1(1)
            sqrt2(0, 1)
            copy_xT(2, 0)
            copy_featT(0)
            act.wait_ge(ld_f0, 16 * 12)
            step(0, 0, 0)
            step(1, 1, 0)
            step(2, 0, 1)
            with act.Fori(1, BATCH - 2) as b:
                step(2 * b + 1, 1, b)
                step(2 * b + 2, 0, b + 1)
            step(GROUPS - 3, 1, BATCH - 2)
            step(GROUPS - 2, 0, BATCH - 1, x_part=False)
            step(GROUPS - 1, 1, BATCH - 1, x_part=False, early=False)
            step(GROUPS, 0, BATCH, x_part=False, early=False, mid=False)

        @block.vector
        def _(dve):
            v = nc.vector
            done = [0]

            def su(ins):
                done[0] += 1
                ins.then_inc(su_v, 1)
                dve.wait_ge(su_v, done[0])

            dve.wait_ge(ld_b, 16)
            su(v.reduce_sum(mean_b[:, :], B_sb[:, :], axis=AX.X))
            su(v.tensor_scalar(mean_b[:, :], mean_b[:, :], 1.0 / D, None, ALU.mult))
            su(v.tensor_scalar(B_sb[:, :], B_sb[:, :], mean_b[:, 0:1], None, ALU.subtract))
            dve.wait_ge(ld_w, 16 * NB)
            su(v.reduce_sum(mean_w[:, :], W4[:, :], axis=AX.X))
            su(v.tensor_scalar(mean_w[:, :], mean_w[:, :], 1.0 / D, None, ALU.mult))
            su(v.tensor_scalar(W4c[:, :], W4[:, :], mean_w[:, 0:1], None, ALU.subtract))
            assert done[0] == SU_CENTRED
            dve.wait_ge(su_t, TS_W)
            v.tensor_copy(BW[:, :, 0:NS], bank[0][:, :].rearrange("p (c k) -> p c k", c=DC))
            v.tensor_copy(BW[:, :, NS:RG], bank[1][:, :].rearrange("p (c k) -> p c k", c=DC)[:, :, 0:BLK])
            su(v.tensor_copy(W4T[:, :, :], bank[1][:, :].rearrange("p (c k) -> p c k", c=DC)))
            assert done[0] == SU_BW
            dve.wait_ge(ld_cls, 16)
            su(v.bn_stats(cls_st[:, :], cls_sb[:, :]))
            su(v.bn_aggr(cls_mv[:, :], cls_st[:, :]))
            su(v.tensor_scalar(cls_ve[:, :], cls_mv[:, 1:2], EPS, None, ALU.add))
            assert done[0] == SU_CLSVE
            dve.wait_ge(su_a, SA_ROOT)
            su(v.reciprocal(cls_r[:, 0:1], cls_sd[:, :]))
            su(v.tensor_tensor(cls_r[:, 1:2], cls_r[:, 0:1], cls_r[:, 0:1], ALU.mult))
            su(v.scalar_tensor_tensor(cls_r[:, 2:3], cls_r[:, 1:2], -0.5, cls_ve[:, :], ALU.mult, ALU.mult))
            su(v.scalar_tensor_tensor(cls_r[:, 3:4], cls_r[:, 2:3], 1.5, cls_r[:, 0:1], ALU.add, ALU.mult))
            su(v.tensor_scalar(cls_n[:, :], cls_sb[:, :], cls_mv[:, 0:1], cls_r[:, 3:4], ALU.subtract, ALU.mult))
            assert done[0] == SU_CLSN
            v.tensor_copy(w_hi[:, :], W4[:, :])
            su(v.tensor_copy(w_x[0:64, :], W4[0:64, :]))
            v.tensor_tensor(w_x[64:P, :], W4[64:P, :], w_hi[64:P, :].bitcast(F32), ALU.subtract)
            dve.wait_ge(su_t, TS_R)
            su(v.tensor_copy(r_all[:, :], bank[2][:, 0:RG]))
            v.tensor_copy(r_hi[:, :], r_all[:, :])
            su(v.tensor_copy(r_x[0:64, :], r_all[0:64, :]))
            su(v.tensor_tensor(r_x[64:P, :], r_all[64:P, :], r_hi[64:P, :].bitcast(F32), ALU.subtract))
            assert done[0] == SU_PARTS
            for c in range(TILES):
                dve.wait_ge(ld_pe[c // 2], 16)
                v.bn_stats(stat_pe[:, c, :], pe_sb[:, c, :])
                dve.wait_ge(su_t, TS_PE + c + 1)
                v.tensor_copy(pe_state[:, c, :], bank[6 + c % 2][:, 0:NS])
                su(v.tensor_scalar(pe_var[:, c, :], bank[6 + c % 2][:, NS:RG], 2.0, None, ALU.mult))
            assert done[0] == SU_PE
            for c in range(TILES):
                ins = v.bn_aggr(var_pe[:, c, :], stat_pe[:, c, :])
            su(ins)
            assert done[0] == SU_VAR
            dve.wait_ge(su_t, TS_CLST)
            su(v.tensor_copy(clsT[:, :], bank[0][:, :]))
            assert done[0] == SU_CLST
            dve.wait_ge(const_step, CONSTS)
            dve.wait_ge(ld_f1, 16 * 8)
            dve.wait_ge(ld_f0, 16 * 12)
            for q in range(2):
                for m in range(2):
                    k, r = 2 * q + m, slice(REM * (2 * q + m), REM * (2 * q + m + 1))
                    v.tensor_copy(spread1[:, q, REM * k:REM * (k + 1)], top1[:, m, P:GE])
                    v.tensor_copy(zf[:, k, m, q:q + 3:2], top0[:, m, 0:2])
                    v.tensor_copy(zf[:, k, m, 4:8].rearrange("p (o d) -> p o d", d=2),
                                  top0[:, m, IN_OP:IN_OP + 2].unsqueeze(2).to_broadcast([P, 2, 2]))
                    v.tensor_copy(zf[:, k, m, 8:9], bias_main[:, 0, m:m + 1])
                    v.tensor_copy(zf[:, 5 + q, m, 8:9], bias_main[:, 1, m:m + 1])
                    v.tensor_copy(zf[r, 4, m, q:q + 3:2], rem0[r, 0:2])
                    v.tensor_copy(zf[r, 4, m, 4:8].rearrange("p (o d) -> p o d", d=2),
                                  rem0[r, IN_OP:IN_OP + 2].unsqueeze(2).to_broadcast([REM, 2, 2]))
                    v.tensor_copy(zf[r, 4, m, 8:9], bias_rem[r, 0:1])
                    v.tensor_copy(zf[r, 7, m, 8:9], bias_rem[r, 1:2]).then_inc(spread_done, 1)
            dve.wait_ge(spread_done, 4)
            v.tensor_copy(zr[:, :, :, 0, :], zf[:, :, :, :]).then_inc(spread_done, 1)
            dve.wait_ge(spread_done, 5)
            v.tensor_tensor(zr[:, :, :, 1, :], zf[:, :, :, :], zr[:, :, :, 0, :].bitcast(F32),
                            ALU.subtract).then_inc(spread_done, 1)
            dve.wait_ge(su_t, TS_CLSU)
            v.tensor_copy(stateT_cls[:, :], bank[3][:, 0:P])
            su(v.tensor_copy(carry_cls[:, :], bank[3][:, 0:1]))
            assert done[0] == SU_CLSU


            def u_1(g, tile0):
                dve.wait_ge(u_ready, g)
                v.tensor_tensor(q_prod[:, 0:3, :], u3[:, :, NS:NS + F], pe_var[:, tile0:tile0 + 3, 0:F], ALU.add)
                v.tensor_tensor(q_prod[:, 3:4, :], u1[:, :, NS:NS + F], pe_var[:, tile0 + 3:tile0 + 4, 0:F], ALU.add
                                ).then_inc(var_read, 1)

            def u_2(g, par):
                dve.wait_ge(var_read, g)
                v.tensor_tensor(q_prod[:, :, :], q_prod[:, :, :], x_in[:, par, :, :], ALU.mult).then_inc(v1[1], 1)

            def u_3(g):
                dve.wait_ge(v1[1], g)
                v.reduce_sum(q_sum[:, :], q_prod[:, :, :], axis=AX.X).then_inc(v1[0], 1)

            def u_4(g, tile0):
                dve.wait_ge(v1[0], g)
                v.scalar_tensor_tensor(ve1[:, :], q_sum[:, :], 1.0 / D, var_pe[:, tile0:tile0 + TPG, 1], ALU.mult, ALU.add
                                       ).then_inc(v1[2], 1)

            def u_5(g):
                dve.wait_ge(v1[2], g)
                v.tensor_scalar(ve1[:, :], ve1[:, :], 0.0, EPS, ALU.max, ALU.add).then_inc(v1[3], 1)

            def u_state(g, tile0):
                v.tensor_tensor(state_raw[:, 3:4, :], u1[:, :, 0:NS], pe_state[:, tile0 + 3:tile0 + 4, :], ALU.add)
                v.tensor_tensor(state_raw[:, 0:3, :], u3[:, :, 0:NS], pe_state[:, tile0:tile0 + 3, :], ALU.add
                                ).then_inc(state_read, 1)

            def newton(k, sems, n, t, sd, ve, nt):
                if k:
                    dve.wait_ge(sems[k - 1], n)
                if k == 0:
                    ins = v.reciprocal(t[:, 0, 0:nt], sd)
                elif k == 1:
                    ins = v.tensor_tensor(t[:, 1, 0:nt], t[:, 0, 0:nt], t[:, 0, 0:nt], ALU.mult)
                elif k == 2:
                    ins = v.scalar_tensor_tensor(t[:, 2, 0:nt], t[:, 1, 0:nt], -0.5, ve, ALU.mult, ALU.mult)
                else:
                    ins = v.scalar_tensor_tensor(t[:, 3, 0:nt], t[:, 2, 0:nt], 1.5, t[:, 0, 0:nt], ALU.add, ALU.mult)
                ins.then_inc(sems[k], 1)

            def newton1(k, g):
                if k == 0:
                    dve.wait_ge(sd1_ready, g)
                newton(k, v1[4:8], g, rs1, sd1[:, :], ve1[:, :], TPG)

            def newton2(k, g, nt):
                if k == 0:
                    dve.wait_ge(sd2_ready, g + 1)
                newton(k, v2[0:4], g + 1, rs2, sd2[:, 0:nt], ve2[:, 0:nt], nt)

            def u_scale(g, tile0, c):
                if c == 0:
                    dve.wait_ge(v1[7], g)
                    after(dve, scan_ready, g - 1)
                ins = v.scalar_tensor_tensor(state_in[:, c, :], state_raw[:, c, :], rs1[:, 3, c:c + 1],
                                             inv_decay[:, tile0 + c, :], ALU.mult, ALU.mult)
                if c == TPG - 1:
                    ins.then_inc(state_scaled, 1)

            def early_b(g, par, tile0):
                start = carry_cls[:, 0:1] if par else carry[:, 1, TPG - 1:TPG]
                after(dve, h_ready[TPG - 1], g - 2)
                dve.wait_ge(scan_ready, g)
                v.tensor_tensor_scan(carry[:, par, :], ones4[:, :], ps_scan[:, P - 1:GT:P], start, ALU.mult, ALU.add
                                     ).then_inc(carry_ready, 1)
                for c in range(TPG):
                    if c == 1:
                        dve.wait_ge(carry_ready, g)
                    ins = v.scalar_tensor_tensor(stateT[:, par, c * P:(c + 1) * P], ps_scan[:, c * P:(c + 1) * P],
                                                 start if c == 0 else carry[:, par, c - 1:c],
                                                 decayT[:, (tile0 + c) * P:(tile0 + c + 1) * P], ALU.add, ALU.mult)
                ins.then_inc(stateT_ready, 1)

            def h_add(g, par, tile0, c):
                if c == 0:
                    after(dve, o_scaled, g - 1)
                dve.wait_ge(h_ready[c], g)
                v.tensor_tensor(h1[:, par, c, :], ps_h[c % 2][:, :], pe_sb[:, tile0 + c, :], ALU.add
                                ).then_inc(h_added[c], 1)

            def h_bn(g, par, c):
                dve.wait_ge(h_added[c], g)
                ins = v.bn_stats(st2[:, c, :], h1[:, par, c, :])
                if c == TPG - 1:
                    ins.then_inc(h_stat, 1)

            def h_aggregate(g, nt):
                v.memset(feat[:, 0:nt, NFEAT - 1:NFEAT].bitcast(F32), 1.0)
                for c in range(nt):
                    ins = v.bn_aggr(mv2[:, c, :], st2[:, c, :])
                ins.then_inc(v2[4], 1)

            def h_eps(g, nt):
                dve.wait_ge(v2[4], g + 1)
                v.tensor_scalar(ve2[:, 0:nt], mv2[:, 0:nt, 1], EPS, None, ALU.add).then_inc(ve2_ready, 1)

            def h_norm(g, par, nt):
                T = slice(0, nt)
                dve.wait_ge(v2[3], g + 1)
                v.tensor_scalar(out_scale[:, par, T], rs2[:, 3, T], 1.0, None, ALU.add)
                v.scalar_tensor_tensor(out_bias[:, par, T], mv2[:, T, 0], -1.0, rs2[:, 3, T], ALU.mult, ALU.mult
                                       ).then_inc(scale_ready, 1)

            def h_y(g, par, nt):
                for c in range(nt):
                    ins = v.tensor_scalar(y[:, c, :], h1[:, par, c, 0:YC], mv2[:, c, 0:1], rs2[:, 3, c:c + 1],
                                          ALU.subtract, ALU.mult)
                ins.then_inc(y_done, 1)

            def features(g, par, nt):
                n, T = g + 1, slice(0, nt)
                dve.wait_ge(y_done, n)
                fields = y[:, T, ALU_LO:ALU_LO + FIELDS * NIB]
                weights = nib_w[:, :, :].rearrange("p f k -> p (f k)").unsqueeze(1).to_broadcast([P, nt, FIELDS * NIB])
                v.scalar_tensor_tensor(first_hit[:, T, :, :].rearrange("p c f k -> p c (f k)"), fields, HALF, weights,
                                       ALU.is_gt, ALU.mult).then_inc(hits_done, 1)
                v.tensor_scalar(marks[:, T, :], y[:, T, 0:3], HALF, None, ALU.is_gt).then_inc(marks_done, 1)
                v.tensor_copy(feat[:, T, 4:8:2], y[:, T, X_OP:X_OP + 2]).then_inc(op_hi_done, 1)
                dve.wait_ge(hits_done, n)
                v.reduce_max(hit_max[:, T, :], first_hit[:, T, :, :], axis=AX.X).then_inc(max_done, 1)
                dve.wait_ge(marks_done, n)
                v.tensor_tensor(both[:, T, :], marks[:, T, 1:3], marks[:, T, 0:1].to_broadcast([P, nt, 2]), ALU.mult
                                ).then_inc(both_done, 1)
                dve.wait_ge(op_hi_done, n)
                v.tensor_tensor(feat[:, T, 5:8:2], y[:, T, X_OP:X_OP + 2], feat[:, T, 4:8:2].bitcast(F32), ALU.subtract)
                dve.wait_ge(max_done, n)
                v.tensor_scalar(hit_pos[:, T, :], hit_max[:, T, :], -1.0, float(NIB), ALU.mult, ALU.add
                                ).then_inc(pos_done, 1)
                dve.wait_ge(both_done, n)
                v.tensor_copy(masks[:, par, T, 0], both[:, T, 0])
                v.tensor_tensor(masks[:, par, T, 1], both[:, T, 1], both[:, T, 0], ALU.is_gt).then_inc(masks_done, 1)
                dve.wait_ge(pos_done, n)
                v.scalar_tensor_tensor(feat[:, T, 0:4], hit_max[:, T, :], 0.0, hit_pos[:, T, :], ALU.is_gt, ALU.mult
                                       ).then_inc(feat_done, 1)
                dve.wait_ge(masks_done, n)
                after(dve, o_done, g - 1)
                v.tensor_tensor(active[:, par, T], masks[:, par, T, 0], masks[:, par, T, 1], ALU.add)
                dve.wait_ge(feat_done, n)
                after(dve, featT_ready, g)
                for m in range(2):
                    ins = v.tensor_tensor(
                        feat_rows[:, T, m * KF // 2:(m + 1) * KF // 2].rearrange("p c (d f) -> p c d f", d=2),
                        feat[:, T, :].bitcast(F32).unsqueeze(2).to_broadcast([P, nt, 2, NFEAT]),
                        masks[:, par, T, m:m + 1].unsqueeze(3).to_broadcast([P, nt, 2, NFEAT]), ALU.mult)
                ins.then_inc(rows_ready, 1)

            def split_y3(s, n):
                dve.wait_ge(y3_parts, s + 1)
                v.tensor_scalar(y3_hi[:, 0:n], ps_small[0:3 * REM, 0:n], b3[:, 0:1], lo_row[:, 0:1], ALU.add, ALU.mult
                                ).then_inc(y3_rounded, 1)
                dve.wait_ge(y3_rounded, s + 1)
                v.scalar_tensor_tensor(y3T[:, 0:n], ps_small[0:3 * REM, 0:n], b3[:, 0:1], y3_hi[:, 0:n].bitcast(F32),
                                       ALU.add, ALU.subtract).then_inc(y3_split, 1)

            def k_step(k, s, par, nt):
                n, T = s + 1, slice(0, nt)
                if k == 0:
                    dve.wait_ge(y3_ready, n)
                    ins = v.tensor_tensor(y3m[:, T, :].rearrange("p c (o m) -> p c o m", m=2),
                                          ps_y[:, T, :].rearrange("p c (o m) -> p c o m", m=2),
                                          masks[:, par, T, :].unsqueeze(2).to_broadcast([P, nt, 3, 2]), ALU.mult)
                    ins.then_inc(p3[0], 1)
                    return
                dve.wait_ge(p3[k - 1], n)
                if k == 1:
                    ins = v.tensor_tensor(res[:, T, :], y3m[:, T, 0:6:2], y3m[:, T, 1:6:2], ALU.add)
                elif k == 2:
                    ins = v.tensor_scalar(res_c[:, T, :], res[:, T, 0:2], 0.0, float(NIB - 1), ALU.max, ALU.min)
                elif k == 3:
                    after(dve, o_done, s)
                    v.tensor_scalar(carry_out[:, T], res[:, T, 2], HALF, None, ALU.is_gt)
                    ins = v.tensor_scalar(res_up[:, T, :], res_c[:, T, :], MAGIC, None, ALU.add)
                elif k == 4:
                    ins = v.tensor_scalar(res_int[:, T, :], res_up[:, T, :], -MAGIC, None, ALU.add)
                else:
                    ins = v.tensor_tensor(is_hot[:, T, :, :],
                                          hot[:, :].unsqueeze(1).unsqueeze(1).to_broadcast([P, nt, 2, NIB]),
                                          res_int[:, T, :].unsqueeze(3).to_broadcast([P, nt, 2, NIB]), ALU.is_equal)
                ins.then_inc(p3[k], 1)

            def step(s, par, early=True, mid=True):
                cls = isinstance(s, int) and s == 0
                nt_before = 1 if isinstance(s, int) and s == 1 else TPG
                mt, et, mp = TPG * par, TPG * (1 - par), 1 - par
                k = lambda n: None if cls else k_step(n, s - 1, 1 - par, nt_before)
                if not cls:
                    split_y3(s - 1, nt_before * P)
                if not mid:
                    for n in range(6):
                        k(n)
                    return
                g = s + 2
                h_add(s + 1, mp, mt, 0)
                h_bn(s + 1, mp, 0)
                h_add(s + 1, mp, mt, 1)
                k(0)
                h_bn(s + 1, mp, 1)
                k(1)
                if early:
                    u_1(g, et)
                k(2)
                if early:
                    u_2(g, par)
                k(3)
                h_add(s + 1, mp, mt, 2)
                k(4)
                if early:
                    u_3(g)
                    u_state(g, et)
                    u_4(g, et)
                k(5)
                if early:
                    u_5(g)
                h_add(s + 1, mp, mt, 3)
                h_bn(s + 1, mp, 2)
                if early:
                    newton1(0, g)
                h_bn(s + 1, mp, 3)
                if early:
                    newton1(1, g)
                dve.wait_ge(h_stat, s + 1)
                h_aggregate(s + 1, TPG)
                if early:
                    newton1(2, g)
                h_eps(s + 1, TPG)
                if early:
                    newton1(3, g)
                for n in range(4):
                    if early:
                        u_scale(g, et, n)
                    newton2(n, s + 1, TPG)
                h_norm(s + 1, mp, TPG)
                h_y(s + 1, mp, TPG)
                features(s + 1, mp, TPG)
                if early:
                    early_b(g, par, et)

            u_1(1, 0)
            u_2(1, 1)
            u_3(1)
            u_4(1, 0)
            u_5(1)
            u_state(1, 0)
            for n in range(4):
                newton1(n, 1)
            dve.wait_ge(decay_ready, 1)
            for c in range(TPG):
                u_scale(1, 0, c)
            dve.wait_ge(su_t, TS_CLSH)
            su(v.tensor_tensor(h1[:, 0, 0, :], bank[4][:, :], cls_sb[:, :], ALU.add))
            assert done[0] == SU_H
            v.bn_stats(st2[:, 0, :], h1[:, 0, 0, :]).then_inc(h_aggr, 1)
            dve.wait_ge(h_aggr, 1)
            h_aggregate(0, 1)
            h_eps(0, 1)
            dve.wait_ge(su_t, TS_FFN)
            v.tensor_copy(w2_main[:, :, :], bank[5][:, 0:2 * P].rearrange("p (m k) -> p m k", m=2))
            v.tensor_copy(w2_main_rem[:, :, :], bank[5][:, 256:256 + 2 * REM].rearrange("p (m k) -> p m k", m=2))
            su(v.tensor_copy(w2_rem[:, :], bank[5][:, 320:320 + P]))
            assert done[0] == SU_ALL
            early_b(1, 1, 0)
            for n in range(4):
                newton2(n, 0, 1)
            h_norm(0, 0, 1)
            h_y(0, 0, 1)
            features(0, 0, 1)
            dve.wait_ge(ld_f3, 16 * 24)
            v.reduce_max(lo_row[:, :], pick_lo[:, :], axis=AX.X).then_inc(l3_step, 1)
            v.tensor_tensor(pick3[:, :], pick_hi[:, :], pick_lo[:, :], ALU.add).then_inc(l3_step, 1)
            v.tensor_copy(w3[:, :, LO_ROW:LO_ROW + 6], w3[:, :, 0:6]).then_inc(l3_step, 1)
            dve.wait_ge(l3_step, 3)
            step(0, 0)
            step(1, 1)
            step(2, 0)
            with dve.Fori(1, BATCH - 1) as b:
                step(2 * b + 1, 1)
                step(2 * b + 2, 0)
            step(GROUPS - 1, 1, early=False)
            step(GROUPS, 0, early=False, mid=False)
            split_y3(GROUPS, GT)
            for n in range(6):
                k_step(n, GROUPS, 0, TPG)

        @block.tensor
        def _(pe_):
            t = nc.tensor
            tile = lambda c: slice(c * P, (c + 1) * P)
            count = [0]

            def su(ins):
                count[0] += 1
                ins.then_inc(su_t, 1)

            pe_.wait_ge(const_step, IDENT)
            pe_.wait_ge(su_v, SU_CENTRED)
            for c in range(DC):
                t.transpose(bank[0][:, tile(c)], B_sb[:, tile(c)], ident[:, :])
            for c in range(DC):
                ins = t.transpose(bank[1][:, tile(c)], W4c[:, tile(c)], ident[:, :])
            su(ins)
            assert count[0] == TS_W
            pe_.wait_ge(ld_c, 16)
            for c in range(DC):
                ins = t.transpose(bank[3][:, tile(c)], C_sb[:, c, :], ident[:, :])
            su(ins)
            assert count[0] == TS_C
            pe_.wait_ge(su_v, SU_BW)
            for c in range(DC):
                ins = t.matmul(bank[2][:, 0:RG], W4T[:, c, :], BW[:, c, :], start=(c == 0), stop=(c == DC - 1))
            su(ins)
            assert count[0] == TS_R
            for k in range(TILES + 1):
                if k < TILES:
                    pe_.wait_ge(ld_pe[k // 2], 16)
                    if k >= 2:
                        pe_.wait_ge(su_a, SA_C + k - 1)
                    for c in range(DC):
                        ins = t.transpose(bank[4 + k % 2][:, tile(c)], pe_sb[:, k, tile(c)], ident[:, :])
                    ins.then_inc(su_tp, 1)
                if k >= 1:
                    pe_.wait_ge(su_a, SA_C + k)
                    if k >= 3:
                        pe_.wait_ge(su_v, SU_PARTS + k - 2)
                    for c in range(DC):
                        ins = t.matmul(bank[6 + (k - 1) % 2][:, 0:RG], peT[:, (k - 1) % 2, tile(c)], BW[:, c, :],
                                       start=(c == 0), stop=(c == DC - 1))
                    su(ins)
            pe_.wait_ge(su_v, SU_CLSN)
            for c in range(DC):
                ins = t.transpose(bank[0][:, tile(c)], cls_n[:, tile(c)], ident[:, :])
            su(ins)
            assert count[0] == TS_CLST
            pe_.wait_ge(const_step, CONSTS)

            def early_x(g, par):
                pe_.wait_ge(x_split, g)
                after(pe_, featT_copied, g - 2)
                for c in range(TPG):
                    ins = t.transpose(ps_T[:, tile(c)], x_parts[:, par, c, :, :].rearrange("p n k -> p (n k)").bitcast(F32),
                                      ident[:, :])
                ins.then_inc(xT_ready, 1)

            def early_u(g, par):
                pe_.wait_ge(xT_copied, g)
                after(pe_, state_read, g - 1)
                after(pe_, p3[0], g - 2)
                for c in range(TPG):
                    ins = t.matmul(u3[:, c, :] if c < 3 else ps_small[:, 0:RG], xT[:, par, tile(c)], r_x[:, :],
                                   start=True, stop=True)
                ins.then_inc(u_ready, 1)

            def early_s(g):
                pe_.wait_ge(state_scaled, g)
                after(pe_, stateT_ready, g - 1)
                for c in range(TPG):
                    ins = t.matmul(ps_scan[:, tile(c)], state_in[:, c, :], tri[:, :], start=True, stop=True)
                ins.then_inc(scan_ready, 1)

            def mid_h(g, par, c):
                if c == 0:
                    pe_.wait_ge(stateT_ready, g)
                if c >= 2:
                    pe_.wait_ge(h_added[c - 2], g)
                else:
                    after(pe_, h_added[c + 2], g - 1)
                t.matmul(ps_h[c % 2][:, :], xT[:, par, tile(c)], w_x[:, :], start=True, stop=False)
                t.matmul(ps_h[c % 2][:, :], stateT[:, par, tile(c)], CT[:, :], start=False, stop=True
                         ).then_inc(h_ready[c], 1)

            def back_f(s, nt):
                pe_.wait_ge(rows_ready, s + 1)
                after(pe_, xT_copied, min(s + 2, GROUPS) if isinstance(s, int) else s + 2)
                for c in range(nt):
                    ins = t.transpose(ps_T[:, tile(c)], feat_rows[:, c, :].bitcast(F32),
                                      ident[:, :])
                ins.then_inc(featT_ready, 1)

            def bank_free(s, k):
                if k >= 2:
                    pe_.wait_ge(f_relu[k - 2], s + 1)
                else:
                    after(pe_, f_relu[k + 6], s)

            def back_1(s, k, n):
                if k == 0:
                    pe_.wait_ge(featT_copied, s + 1)
                bank_free(s, k)
                t.matmul(ps_f[k % 2][:, 0:n], w_feat[:, k, :], featT[:, 0:n], start=True, stop=True).then_inc(f_ready[k], 1)

            def back_2(s, q, n):
                k = 5 + q
                bank_free(s, k)
                o = ps_f[k % 2][:, 0:n]
                t.matmul(o, w_feat[:, k, :], featT[:, 0:n], start=True, stop=False)
                for m in range(2):
                    t.matmul(o, w2_main[:, m, :], hid1[:, 2 * q + m, 0:n], start=False, stop=False)
                pe_.wait_ge(f_relu[4], s + 1)
                t.matmul(o, w2_rem_main[:, q, :], hid1[:, 4, 0:n], start=False, stop=True).then_inc(f_ready[k], 1)

            def back_2r(s, n):
                bank_free(s, 7)
                o = ps_f[1][:, 0:n]
                t.matmul(o, w2_rem[:, :], hid1[:, 4, 0:n], start=True, stop=False)
                for k in range(4):
                    ins = t.matmul(ps_f[1][REM * k:REM * (k + 1), 0:n], w2_main_rem[:, k % 2, :], hid1[:, k, 0:n],
                                   start=False, stop=True)
                ins.then_inc(f_ready[7], 1)

            def back_3(s, n, early_g):
                pe_.wait_ge(f_relu[7], s + 1)
                after(pe_, state_read, early_g)
                after(pe_, p3[0], s)
                for k in range(3):
                    ins = t.matmul(ps_small[REM * k:REM * (k + 1), 0:n], w3[:, k, :], hid2[:, k, 0:n], start=True, stop=True)
                ins.then_inc(y3_parts, 1)

            def back_4(s, nt):
                pe_.wait_ge(y3_split, s + 1)
                for c in range(nt):
                    ins = t.matmul(ps_y[:, c, :], y3T[:, tile(c)], pick3[:, :], start=True, stop=True)
                ins.then_inc(y3_ready, 1)

            def step(s, par, x_part=True, early=True, mid=True):
                cls = isinstance(s, int) and s == 0
                n = P if cls else GT
                if cls:
                    mid_h(1, 1, 0)
                    mid_h(1, 1, 1)
                    back_f(0, 1)
                    pe_.wait_ge(su_v, SU_ALL)
                    pe_.wait_ge(l3_step, 3)
                back_1(s, 0, n)
                back_1(s, 1, n)
                if not cls:
                    if mid:
                        mid_h(s + 1, 1 - par, 0)
                        mid_h(s + 1, 1 - par, 1)
                    back_4(s - 1, 1 if isinstance(s, int) and s == 1 else TPG)
                if mid:
                    mid_h(s + 1, 1 - par, 2)
                if early:
                    early_u(s + 2, par)
                back_1(s, 2, n)
                back_1(s, 3, n)
                if mid:
                    mid_h(s + 1, 1 - par, 3)
                back_1(s, 4, n)
                back_2(s, 0, n)
                back_2(s, 1, n)
                if x_part:
                    early_x(s + 3, 1 - par)
                back_2r(s, n)
                if early:
                    early_s(s + 2)
                if mid:
                    back_f(s + 1, TPG)
                back_3(s, n, s + 2 if early else GROUPS)

            pe_.wait_ge(su_v, SU_CLST)
            for c in range(DC):
                ins = t.matmul(bank[3][:, 0:P], BW[:, c, 0:NS], clsT[:, tile(c)], start=(c == 0), stop=(c == DC - 1))
            su(ins)
            assert count[0] == TS_CLSU
            early_x(1, 1)
            early_u(1, 1)
            pe_.wait_ge(ld_f1, 16 * 8)
            pe_.wait_ge(spread_done, 6)
            pe_.wait_ge(su_v, SU_PE)
            for m in range(2):
                t.transpose(bank[5][:, tile(m)], top1[:, m, 0:P], ident[:, :])
                t.transpose(bank[5][:, 256 + REM * m:256 + REM * (m + 1)], bot1[:, m, 0:P], ident[0:REM, 0:REM])
                t.transpose(bank[4][:, tile(m)], spread1[:, m, :], ident[:, :])
            t.transpose(bank[5][:, 320:320 + P], diag1[:, :], ident[:, :])
            for k in range(8):
                ins = t.transpose(bank[6 + k // 4][0:KF, tile(k % 4)],
                                  zr[:, k, :, :, :].rearrange("p m d f -> p (m d f)").bitcast(F32), ident[:, :])
            su(ins)
            assert count[0] == TS_FFN
            pe_.wait_ge(su_v, SU_CLSU)
            pe_.wait_ge(su_a, SA_REM)
            su(t.matmul(bank[4][:, :], stateT_cls[:, :], CT[:, :], start=True, stop=True))
            assert count[0] == TS_CLSH
            early_s(1)
            early_x(2, 0)
            step(0, 0)
            step(1, 1)
            step(2, 0)
            with pe_.Fori(1, BATCH - 2) as b:
                step(2 * b + 1, 1)
                step(2 * b + 2, 0)
            step(GROUPS - 3, 1)
            step(GROUPS - 2, 0, x_part=False)
            step(GROUPS - 1, 1, x_part=False, early=False)
            step(GROUPS, 0, x_part=False, early=False, mid=False)
            back_4(GROUPS, TPG)


_INS = ["x", "cls_tok", "L0_tok_W", "L0_attn_log_lambda", "L0_attn_B", "L0_attn_C", "L0_attn_log_dt",
        "L0_ffn_Wa", "L0_ffn_ba", "L0_ffn_Ws", "L0_ffn_bs"]


def kernel(**inputs):
    import concourse.bacc as bacc
    from concourse.bass_utils import run_bass_kernel_spmd

    nc = bacc.Bacc("TRN2", target_bir_lowering=False, num_devices=1)
    arrays, args = {}, []

    def give(name, a):
        arrays[name] = a
        args.append(nc.dram_tensor(name, a.shape, mybir.dt.from_np(a.dtype), kind="ExternalInput").ap())

    for name in _INS:
        a = np.ascontiguousarray(inputs[name])
        give(f"in_{name}", a.reshape(1) if a.ndim == 0 else a)
    batch, height, width, _ = arrays["in_x"].shape
    d_model = arrays["in_L0_tok_W"].shape[1]
    give("pe", position_table(height * width, d_model))
    out = nc.dram_tensor("out", (batch, height * width + 1, d_model), F32, kind="ExternalOutput").ap()
    vit_layer(nc, *args, out)
    r = run_bass_kernel_spmd(nc, [arrays], core_ids=[0])
    return r.results[0]["out"]
```
